# Optimizing a Trainium2 kernel written in Bass

```python
import numpy as np
import jax
import jax.numpy as jnp

def _softmax(x, axis=-1):
    return jax.nn.softmax(x, axis=axis)
def _gelu(x):
    return jax.nn.gelu(x, approximate=True)
def _silu(x):
    return jax.nn.silu(x)
def _sigmoid(x):
    return jax.nn.sigmoid(x)
def _layernorm(x, axis=-1, eps=1e-5):
    m = jnp.mean(x, axis=axis, keepdims=True)
    v = jnp.var(x, axis=axis, keepdims=True)
    return (x - m) / jnp.sqrt(v + eps)
def _scatter_add(tgt, idx, src, axis=0):
    return tgt.at[idx].add(src)
def _segment_sum(src, seg, n):
    return jax.ops.segment_sum(src, seg, n)

kernel_name = 'mk_conv_seq_d4_conv_nchw256_510228'

def setup_inputs(seed: int = 0):
    np.random.seed(seed)
    _w = jnp.asarray
    def _rec_inputs():
        import jax
        import jax.numpy as jnp
        _gk = jax.random.key(seed)
        x = -0.0005207 + 1.001 * jax.random.normal(jax.random.fold_in(_gk, 1), (2, 256, 64, 64), jnp.float32)
        return x
    x = _rec_inputs()
    def _L0_conv_setup():
        import jax, jax.numpy as jnp
        import numpy as np
        NUM_HEADS = 4
        GROUPS = 8
        EPS = 1e-05

        def group_norm(x, gamma, beta):
            B, C, H, W = x.shape
            xg = x.reshape(B, GROUPS, C // GROUPS, H, W)
            mean = xg.mean(axis=(2, 3, 4), keepdims=True)
            var = xg.var(axis=(2, 3, 4), keepdims=True)
            xn = ((xg - mean) * jax.lax.rsqrt(var + EPS)).reshape(B, C, H, W)
            return xn * gamma[None, :, None, None] + beta[None, :, None, None]
        key = jax.random.key(seed)
        k1, k2, k3 = jax.random.split(key, 3)
        B, C, H, W = (2, 256, 64, 64)
        x = jax.random.normal(k1, (B, C, H, W), dtype=jnp.float32)
        gn_gamma = jnp.ones((C,), dtype=jnp.float32)
        gn_beta = jnp.zeros((C,), dtype=jnp.float32)
        w_qkv = jax.random.normal(k2, (3 * C, C), dtype=jnp.float32) * C ** (-0.5)
        w_proj = jax.random.normal(k3, (C, C), dtype=jnp.float32) * C ** (-0.5)
        b_proj = jnp.zeros((C,), dtype=jnp.float32)
        return {'x': x, 'gn_gamma': gn_gamma, 'gn_beta': gn_beta, 'w_qkv': w_qkv, 'w_proj': w_proj, 'b_proj': b_proj}
    _L0_conv_all = _L0_conv_setup()
    _L0_conv_in = {k: v for k, v in _L0_conv_all.items() if k in ('gn_gamma', 'gn_beta', 'w_qkv', 'w_proj', 'b_proj', )}
    del _L0_conv_all

    def _L1_conv_setup():
        import jax, jax.numpy as jnp
        import numpy as np
        B, C, H, Wd = (32, 256, 64, 64)
        key = jax.random.key(seed)
        k1, k2, k3 = jax.random.split(key, 3)
        x = jax.random.normal(k1, (B, C, H, Wd), dtype=jnp.float32)
        W = jax.random.normal(k2, (C, 4), dtype=jnp.float32) * 0.5
        b = jax.random.normal(k3, (C,), dtype=jnp.float32) * 0.1
        return {'x': x, 'W': W, 'b': b}
    _L1_conv_all = _L1_conv_setup()
    _L1_conv_in = {k: v for k, v in _L1_conv_all.items() if k in ('W', 'b', )}
    del _L1_conv_all

    def _L2_conv_setup():
        import jax, jax.numpy as jnp
        import numpy as np
        EPS = 1e-05

        def _bn(x, g, b, m, v):
            s = g / jnp.sqrt(v + EPS)
            return x * s[None, :, None, None] + (b - m * s)[None, :, None, None]

        def _conv1x1(x, w):
            return jnp.einsum('bchw,oc->bohw', x, w)

        def _bilinear(img, y, x):
            B, C, Hi, Wi = img.shape
            y0 = jnp.floor(y)
            x0 = jnp.floor(x)
            wy1 = y - y0
            wx1 = x - x0
            wy0 = 1.0 - wy1
            wx0 = 1.0 - wx1
            imgf = img.reshape(B, C, Hi * Wi)

            def gather(yi, xi):
                valid = (yi >= 0) & (yi < Hi) & (xi >= 0) & (xi < Wi)
                yc = jnp.clip(yi, 0, Hi - 1).astype(jnp.int32)
                xc = jnp.clip(xi, 0, Wi - 1).astype(jnp.int32)
                flat = yc * Wi + xc

                def per_b(imgb, flatb):
                    return imgb[:, flatb.reshape(-1)].reshape(C, *flatb.shape)
                out = jax.vmap(per_b)(imgf, flat)
                return out * valid[:, None].astype(img.dtype)
            return gather(y0, x0) * (wy0 * wx0)[:, None] + gather(y0, x0 + 1) * (wy0 * wx1)[:, None] + gather(y0 + 1, x0) * (wy1 * wx0)[:, None] + gather(y0 + 1, x0 + 1) * (wy1 * wx1)[:, None]

        def _dcn(h, woff, boff, w2, b2):
            B, C, H, W = h.shape
            off = jax.lax.conv_general_dilated(h, woff, (1, 1), [(1, 1), (1, 1)], dimension_numbers=('NCHW', 'OIHW', 'NCHW')) + boff[None, :, None, None]
            o = off[:, :18].reshape(B, 9, 2, H, W)
            mask = jax.nn.sigmoid(off[:, 18:])
            ky, kx = jnp.meshgrid(jnp.arange(3), jnp.arange(3), indexing='ij')
            base_y = (jnp.arange(H)[None, :, None] - 1 + ky.reshape(9)[:, None, None]).astype(h.dtype)
            base_x = (jnp.arange(W)[None, None, :] - 1 + kx.reshape(9)[:, None, None]).astype(h.dtype)
            y = o[:, :, 0] + base_y[None]
            x = o[:, :, 1] + base_x[None]
            samp = _bilinear(h, y, x) * mask[:, None]
            out = jnp.einsum('bckhw,ock->bohw', samp, w2.reshape(w2.shape[0], w2.shape[1], 9))
            return out + b2[None, :, None, None]
        key = jax.random.key(seed)
        ks = jax.random.split(key, 20)
        B, Cin, Cb, H, W = (4, 256, 64, 112, 112)
        d = {'x': jax.random.normal(ks[0], (B, Cin, H, W), jnp.float32), 'w1': jax.random.normal(ks[1], (Cb, Cin), jnp.float32) * 0.05, 'bn1_g': jax.random.uniform(ks[2], (Cb,), jnp.float32, 0.5, 1.5), 'bn1_b': jax.random.normal(ks[3], (Cb,), jnp.float32) * 0.1, 'bn1_m': jax.random.normal(ks[4], (Cb,), jnp.float32) * 0.1, 'bn1_v': jax.random.uniform(ks[5], (Cb,), jnp.float32, 0.5, 1.5), 'woff': jax.random.normal(ks[6], (27, Cb, 3, 3), jnp.float32) * 0.01, 'boff': jax.random.normal(ks[7], (27,), jnp.float32) * 0.1, 'w2': jax.random.normal(ks[8], (Cb, Cb, 3, 3), jnp.float32) * 0.05, 'dcn_b': jax.random.normal(ks[9], (Cb,), jnp.float32) * 0.1, 'bn2_g': jax.random.uniform(ks[10], (Cb,), jnp.float32, 0.5, 1.5), 'bn2_b': jax.random.normal(ks[11], (Cb,), jnp.float32) * 0.1, 'bn2_m': jax.random.normal(ks[12], (Cb,), jnp.float32) * 0.1, 'bn2_v': jax.random.uniform(ks[13], (Cb,), jnp.float32, 0.5, 1.5), 'w3': jax.random.normal(ks[14], (Cin, Cb), jnp.float32) * 0.05, 'bn3_g': jax.random.uniform(ks[15], (Cin,), jnp.float32, 0.5, 1.5), 'bn3_b': jax.random.normal(ks[16], (Cin,), jnp.float32) * 0.1, 'bn3_m': jax.random.normal(ks[17], (Cin,), jnp.float32) * 0.1, 'bn3_v': jax.random.uniform(ks[18], (Cin,), jnp.float32, 0.5, 1.5)}
        return d
    _L2_conv_all = _L2_conv_setup()
    _L2_conv_in = {k: v for k, v in _L2_conv_all.items() if k in ('w1', 'bn1_g', 'bn1_b', 'bn1_m', 'bn1_v', 'woff', 'boff', 'w2', 'dcn_b', 'bn2_g', 'bn2_b', 'bn2_m', 'bn2_v', 'w3', 'bn3_g', 'bn3_b', 'bn3_m', 'bn3_v', )}
    del _L2_conv_all

    def _L3_conv_setup():
        import jax, jax.numpy as jnp
        import numpy as np
        from jax import lax
        EPS = 1e-05
        NUM_GROUPS = 32
        OFFSET_SCALE = 1.0
        K = 3
        KK = K * K
        DWK = 7

        def group_norm(x, gamma, beta, num_groups=NUM_GROUPS):
            B, C, H, W = x.shape
            xg = x.reshape(B, num_groups, C // num_groups, H, W)
            m = xg.mean(axis=(2, 3, 4), keepdims=True)
            v = xg.var(axis=(2, 3, 4), keepdims=True)
            xn = ((xg - m) * lax.rsqrt(v + EPS)).reshape(B, C, H, W)
            return xn * gamma[None, :, None, None] + beta[None, :, None, None]

        def bilinear_gather(x, py, px):
            B, C, H, W = x.shape
            y0 = jnp.floor(py)
            x0 = jnp.floor(px)
            wy1 = py - y0
            wx1 = px - x0
            wy0 = 1.0 - wy1
            wx0 = 1.0 - wx1
            xf = x.reshape(B, C, H * W)

            def gather(yi, xi):
                valid = (yi >= 0) & (yi <= H - 1) & (xi >= 0) & (xi <= W - 1)
                yc = jnp.clip(yi, 0, H - 1).astype(jnp.int32)
                xc = jnp.clip(xi, 0, W - 1).astype(jnp.int32)
                idx = (yc * W + xc).reshape(B, -1)
                g = jax.vmap(lambda a, i: a[:, i])(xf, idx)
                g = g.reshape(B, C, KK, H, W)
                return g * valid.astype(x.dtype)[:, None]
            out = gather(y0, x0) * (wy0 * wx0)[:, None] + gather(y0, x0 + 1.0) * (wy0 * wx1)[:, None] + gather(y0 + 1.0, x0) * (wy1 * wx0)[:, None] + gather(y0 + 1.0, x0 + 1.0) * (wy1 * wx1)[:, None]
            return out

        def deform_conv(x, dw, pw, pwb, w, b):
            B, C, H, W = x.shape
            dn = ('NCHW', 'OIHW', 'NCHW')
            f = lax.conv_general_dilated(x, dw, (1, 1), 'SAME', feature_group_count=C, dimension_numbers=dn)
            off = lax.conv_general_dilated(f, pw, (1, 1), 'SAME', dimension_numbers=dn)
            off = (off + pwb[None, :, None, None]) * OFFSET_SCALE
            off = off.reshape(B, KK, 2, H, W)
            ks = jnp.arange(K, dtype=x.dtype) - (K - 1) / 2
            ky = jnp.repeat(ks, K)
            kx = jnp.tile(ks, K)
            yy, xx = jnp.meshgrid(jnp.arange(H, dtype=x.dtype), jnp.arange(W, dtype=x.dtype), indexing='ij')
            py = yy[None, None] + ky[None, :, None, None] + off[:, :, 0]
            px = xx[None, None] + kx[None, :, None, None] + off[:, :, 1]
            sampled = bilinear_gather(x, py, px)
            O = w.shape[0]
            out = jnp.einsum('bckhw,ock->bohw', sampled, w.reshape(O, C, KK))
            return out + b[None, :, None, None]
        key = jax.random.key(seed)
        ks = jax.random.split(key, 10)
        B, C, H, W = (4, 256, 64, 64)
        O = C
        x = jax.random.normal(ks[0], (B, C, H, W), dtype=jnp.float32)

        def conv_w(k, shape, fan_in):
            return jax.random.normal(k, shape, dtype=jnp.float32) / np.sqrt(fan_in)
        inp = {'x': x, 'gn1_g': jnp.ones((C,), jnp.float32), 'gn1_b': jnp.zeros((C,), jnp.float32), 'dw1': conv_w(ks[1], (C, 1, DWK, DWK), DWK * DWK), 'pw1': jax.random.normal(ks[2], (2 * KK, C, 1, 1), jnp.float32) * 0.01, 'pwb1': jnp.zeros((2 * KK,), jnp.float32), 'w1': conv_w(ks[3], (O, C, K, K), C * KK), 'b1': jnp.zeros((O,), jnp.float32), 'gn2_g': jnp.ones((O,), jnp.float32), 'gn2_b': jnp.zeros((O,), jnp.float32), 'dw2': conv_w(ks[4], (O, 1, DWK, DWK), DWK * DWK), 'pw2': jax.random.normal(ks[5], (2 * KK, O, 1, 1), jnp.float32) * 0.01, 'pwb2': jnp.zeros((2 * KK,), jnp.float32), 'w2': conv_w(ks[6], (O, O, K, K), O * KK), 'b2': jnp.zeros((O,), jnp.float32)}
        return inp
    _L3_conv_all = _L3_conv_setup()
    _L3_conv_in = {k: v for k, v in _L3_conv_all.items() if k in ('gn1_g', 'gn1_b', 'dw1', 'pw1', 'pwb1', 'w1', 'b1', 'gn2_g', 'gn2_b', 'dw2', 'pw2', 'pwb2', 'w2', 'b2', )}
    del _L3_conv_all

    return {
        "x": x,
        "L0_conv_gn_gamma": _L0_conv_in["gn_gamma"],
        "L0_conv_gn_beta": _L0_conv_in["gn_beta"],
        "L0_conv_w_qkv": _L0_conv_in["w_qkv"],
        "L0_conv_w_proj": _L0_conv_in["w_proj"],
        "L0_conv_b_proj": _L0_conv_in["b_proj"],
        "L1_conv_W": _L1_conv_in["W"],
        "L1_conv_b": _L1_conv_in["b"],
        "L2_conv_w1": _L2_conv_in["w1"],
        "L2_conv_bn1_g": _L2_conv_in["bn1_g"],
        "L2_conv_bn1_b": _L2_conv_in["bn1_b"],
        "L2_conv_bn1_m": _L2_conv_in["bn1_m"],
        "L2_conv_bn1_v": _L2_conv_in["bn1_v"],
        "L2_conv_woff": _L2_conv_in["woff"],
        "L2_conv_boff": _L2_conv_in["boff"],
        "L2_conv_w2": _L2_conv_in["w2"],
        "L2_conv_dcn_b": _L2_conv_in["dcn_b"],
        "L2_conv_bn2_g": _L2_conv_in["bn2_g"],
        "L2_conv_bn2_b": _L2_conv_in["bn2_b"],
        "L2_conv_bn2_m": _L2_conv_in["bn2_m"],
        "L2_conv_bn2_v": _L2_conv_in["bn2_v"],
        "L2_conv_w3": _L2_conv_in["w3"],
        "L2_conv_bn3_g": _L2_conv_in["bn3_g"],
        "L2_conv_bn3_b": _L2_conv_in["bn3_b"],
        "L2_conv_bn3_m": _L2_conv_in["bn3_m"],
        "L2_conv_bn3_v": _L2_conv_in["bn3_v"],
        "L3_conv_gn1_g": _L3_conv_in["gn1_g"],
        "L3_conv_gn1_b": _L3_conv_in["gn1_b"],
        "L3_conv_dw1": _L3_conv_in["dw1"],
        "L3_conv_pw1": _L3_conv_in["pw1"],
        "L3_conv_pwb1": _L3_conv_in["pwb1"],
        "L3_conv_w1": _L3_conv_in["w1"],
        "L3_conv_b1": _L3_conv_in["b1"],
        "L3_conv_gn2_g": _L3_conv_in["gn2_g"],
        "L3_conv_gn2_b": _L3_conv_in["gn2_b"],
        "L3_conv_dw2": _L3_conv_in["dw2"],
        "L3_conv_pw2": _L3_conv_in["pw2"],
        "L3_conv_pwb2": _L3_conv_in["pwb2"],
        "L3_conv_w2": _L3_conv_in["w2"],
        "L3_conv_b2": _L3_conv_in["b2"],
    }

def reference(x, L0_conv_gn_gamma, L0_conv_gn_beta, L0_conv_w_qkv, L0_conv_w_proj, L0_conv_b_proj, L1_conv_W, L1_conv_b, L2_conv_w1, L2_conv_bn1_g, L2_conv_bn1_b, L2_conv_bn1_m, L2_conv_bn1_v, L2_conv_woff, L2_conv_boff, L2_conv_w2, L2_conv_dcn_b, L2_conv_bn2_g, L2_conv_bn2_b, L2_conv_bn2_m, L2_conv_bn2_v, L2_conv_w3, L2_conv_bn3_g, L2_conv_bn3_b, L2_conv_bn3_m, L2_conv_bn3_v, L3_conv_gn1_g, L3_conv_gn1_b, L3_conv_dw1, L3_conv_pw1, L3_conv_pwb1, L3_conv_w1, L3_conv_b1, L3_conv_gn2_g, L3_conv_gn2_b, L3_conv_dw2, L3_conv_pw2, L3_conv_pwb2, L3_conv_w2, L3_conv_b2):
    import jax
    import jax.numpy as jnp
    def _L0_conv_ref(x, gn_gamma, gn_beta, w_qkv, w_proj, b_proj):
        import jax, jax.numpy as jnp
        import numpy as np
        NUM_HEADS = 4
        GROUPS = 8
        EPS = 1e-05

        def group_norm(x, gamma, beta):
            B, C, H, W = x.shape
            xg = x.reshape(B, GROUPS, C // GROUPS, H, W)
            mean = xg.mean(axis=(2, 3, 4), keepdims=True)
            var = xg.var(axis=(2, 3, 4), keepdims=True)
            xn = ((xg - mean) * jax.lax.rsqrt(var + EPS)).reshape(B, C, H, W)
            return xn * gamma[None, :, None, None] + beta[None, :, None, None]
        B, C, H, W = x.shape
        nh = NUM_HEADS
        d = C // nh
        xn = group_norm(x, gn_gamma, gn_beta)
        qkv = jnp.einsum('bchw,oc->bohw', xn, w_qkv).reshape(B, 3, nh, d, H * W)
        q, k, v = (qkv[:, 0], qkv[:, 1], qkv[:, 2])
        scores = jnp.einsum('bhci,bhcj->bhij', q, k) * d ** (-0.5)
        attn = jax.nn.softmax(scores, axis=-1)
        out = jnp.einsum('bhij,bhcj->bhci', attn, v).reshape(B, C, H, W)
        proj = jnp.einsum('bchw,oc->bohw', out, w_proj) + b_proj[None, :, None, None]
        return xn + proj

    def _L1_conv_ref(x, W, b):
        import jax, jax.numpy as jnp
        import numpy as np
        B, C, H, Wd = (32, 256, 64, 64)
        batch, ch, h, w = x.shape
        jj = (jnp.arange(w, dtype=x.dtype) / (w - 1))[None, :]
        ii = (jnp.arange(h, dtype=x.dtype) / (h - 1))[:, None]
        pos = jnp.stack([jnp.broadcast_to(jj, (h, w)), jnp.broadcast_to(ii, (h, w)), jnp.broadcast_to(1.0 - jj, (h, w)), jnp.broadcast_to(1.0 - ii, (h, w))], axis=-1)
        pe = pos @ W.T + b
        pe = jnp.broadcast_to(pe[None], (batch, h, w, ch)).reshape(batch, ch, h, w)
        return x + pe

    def _L2_conv_ref(x, w1, bn1_g, bn1_b, bn1_m, bn1_v, woff, boff, w2, dcn_b, bn2_g, bn2_b, bn2_m, bn2_v, w3, bn3_g, bn3_b, bn3_m, bn3_v):
        import jax, jax.numpy as jnp
        import numpy as np
        EPS = 1e-05

        def _bn(x, g, b, m, v):
            s = g / jnp.sqrt(v + EPS)
            return x * s[None, :, None, None] + (b - m * s)[None, :, None, None]

        def _conv1x1(x, w):
            return jnp.einsum('bchw,oc->bohw', x, w)

        def _bilinear(img, y, x):
            B, C, Hi, Wi = img.shape
            y0 = jnp.floor(y)
            x0 = jnp.floor(x)
            wy1 = y - y0
            wx1 = x - x0
            wy0 = 1.0 - wy1
            wx0 = 1.0 - wx1
            imgf = img.reshape(B, C, Hi * Wi)

            def gather(yi, xi):
                valid = (yi >= 0) & (yi < Hi) & (xi >= 0) & (xi < Wi)
                yc = jnp.clip(yi, 0, Hi - 1).astype(jnp.int32)
                xc = jnp.clip(xi, 0, Wi - 1).astype(jnp.int32)
                flat = yc * Wi + xc

                def per_b(imgb, flatb):
                    return imgb[:, flatb.reshape(-1)].reshape(C, *flatb.shape)
                out = jax.vmap(per_b)(imgf, flat)
                return out * valid[:, None].astype(img.dtype)
            return gather(y0, x0) * (wy0 * wx0)[:, None] + gather(y0, x0 + 1) * (wy0 * wx1)[:, None] + gather(y0 + 1, x0) * (wy1 * wx0)[:, None] + gather(y0 + 1, x0 + 1) * (wy1 * wx1)[:, None]

        def _dcn(h, woff, boff, w2, b2):
            B, C, H, W = h.shape
            off = jax.lax.conv_general_dilated(h, woff, (1, 1), [(1, 1), (1, 1)], dimension_numbers=('NCHW', 'OIHW', 'NCHW')) + boff[None, :, None, None]
            o = off[:, :18].reshape(B, 9, 2, H, W)
            mask = jax.nn.sigmoid(off[:, 18:])
            ky, kx = jnp.meshgrid(jnp.arange(3), jnp.arange(3), indexing='ij')
            base_y = (jnp.arange(H)[None, :, None] - 1 + ky.reshape(9)[:, None, None]).astype(h.dtype)
            base_x = (jnp.arange(W)[None, None, :] - 1 + kx.reshape(9)[:, None, None]).astype(h.dtype)
            y = o[:, :, 0] + base_y[None]
            x = o[:, :, 1] + base_x[None]
            samp = _bilinear(h, y, x) * mask[:, None]
            out = jnp.einsum('bckhw,ock->bohw', samp, w2.reshape(w2.shape[0], w2.shape[1], 9))
            return out + b2[None, :, None, None]
        h = jax.nn.relu(_bn(_conv1x1(x, w1), bn1_g, bn1_b, bn1_m, bn1_v))
        h = _dcn(h, woff, boff, w2, dcn_b)
        h = jax.nn.relu(_bn(h, bn2_g, bn2_b, bn2_m, bn2_v))
        h = _bn(_conv1x1(h, w3), bn3_g, bn3_b, bn3_m, bn3_v)
        return jax.nn.relu(h + x)

    def _L3_conv_ref(x, gn1_g, gn1_b, dw1, pw1, pwb1, w1, b1, gn2_g, gn2_b, dw2, pw2, pwb2, w2, b2):
        import jax, jax.numpy as jnp
        import numpy as np
        from jax import lax
        EPS = 1e-05
        NUM_GROUPS = 32
        OFFSET_SCALE = 1.0
        K = 3
        KK = K * K
        DWK = 7

        def group_norm(x, gamma, beta, num_groups=NUM_GROUPS):
            B, C, H, W = x.shape
            xg = x.reshape(B, num_groups, C // num_groups, H, W)
            m = xg.mean(axis=(2, 3, 4), keepdims=True)
            v = xg.var(axis=(2, 3, 4), keepdims=True)
            xn = ((xg - m) * lax.rsqrt(v + EPS)).reshape(B, C, H, W)
            return xn * gamma[None, :, None, None] + beta[None, :, None, None]

        def bilinear_gather(x, py, px):
            B, C, H, W = x.shape
            y0 = jnp.floor(py)
            x0 = jnp.floor(px)
            wy1 = py - y0
            wx1 = px - x0
            wy0 = 1.0 - wy1
            wx0 = 1.0 - wx1
            xf = x.reshape(B, C, H * W)

            def gather(yi, xi):
                valid = (yi >= 0) & (yi <= H - 1) & (xi >= 0) & (xi <= W - 1)
                yc = jnp.clip(yi, 0, H - 1).astype(jnp.int32)
                xc = jnp.clip(xi, 0, W - 1).astype(jnp.int32)
                idx = (yc * W + xc).reshape(B, -1)
                g = jax.vmap(lambda a, i: a[:, i])(xf, idx)
                g = g.reshape(B, C, KK, H, W)
                return g * valid.astype(x.dtype)[:, None]
            out = gather(y0, x0) * (wy0 * wx0)[:, None] + gather(y0, x0 + 1.0) * (wy0 * wx1)[:, None] + gather(y0 + 1.0, x0) * (wy1 * wx0)[:, None] + gather(y0 + 1.0, x0 + 1.0) * (wy1 * wx1)[:, None]
            return out

        def deform_conv(x, dw, pw, pwb, w, b):
            B, C, H, W = x.shape
            dn = ('NCHW', 'OIHW', 'NCHW')
            f = lax.conv_general_dilated(x, dw, (1, 1), 'SAME', feature_group_count=C, dimension_numbers=dn)
            off = lax.conv_general_dilated(f, pw, (1, 1), 'SAME', dimension_numbers=dn)
            off = (off + pwb[None, :, None, None]) * OFFSET_SCALE
            off = off.reshape(B, KK, 2, H, W)
            ks = jnp.arange(K, dtype=x.dtype) - (K - 1) / 2
            ky = jnp.repeat(ks, K)
            kx = jnp.tile(ks, K)
            yy, xx = jnp.meshgrid(jnp.arange(H, dtype=x.dtype), jnp.arange(W, dtype=x.dtype), indexing='ij')
            py = yy[None, None] + ky[None, :, None, None] + off[:, :, 0]
            px = xx[None, None] + kx[None, :, None, None] + off[:, :, 1]
            sampled = bilinear_gather(x, py, px)
            O = w.shape[0]
            out = jnp.einsum('bckhw,ock->bohw', sampled, w.reshape(O, C, KK))
            return out + b[None, :, None, None]
        h = jax.nn.relu(group_norm(x, gn1_g, gn1_b))
        h = deform_conv(h, dw1, pw1, pwb1, w1, b1)
        h = jax.nn.relu(group_norm(h, gn2_g, gn2_b))
        h = deform_conv(h, dw2, pw2, pwb2, w2, b2)
        return h + x

    def _gn(v, G=32, eps=1e-5):
        B_, C_, H_, W_ = v.shape
        g = v.reshape(B_, G, C_ // G, H_, W_)
        m = jnp.mean(g, axis=(2, 3, 4), keepdims=True)
        s = jnp.var(g, axis=(2, 3, 4), keepdims=True)
        return ((g - m) / jnp.sqrt(s + eps)).reshape(v.shape)

    def _ln_c(v, eps=1e-6):
        m = jnp.mean(v, axis=1, keepdims=True)
        s = jnp.var(v, axis=1, keepdims=True)
        return (v - m) / jnp.sqrt(s + eps)

    def _ln_t(v, eps=1e-5):
        m = jnp.mean(v, axis=-1, keepdims=True)
        s = jnp.var(v, axis=-1, keepdims=True)
        return (v - m) / jnp.sqrt(s + eps)

    def _to_tokens(v):
        B_, C_, H_, W_ = v.shape
        return v.reshape(B_, C_, H_ * W_).transpose(0, 2, 1)
    def _from_tokens(t, like):
        B_, C_, H_, W_ = like.shape
        return t.transpose(0, 2, 1).reshape(B_, C_, H_, W_)

    x = _L0_conv_ref(x, L0_conv_gn_gamma, L0_conv_gn_beta, L0_conv_w_qkv, L0_conv_w_proj, L0_conv_b_proj)
    x = _L1_conv_ref(x, L1_conv_W, L1_conv_b)
    x = _L2_conv_ref(x, L2_conv_w1, L2_conv_bn1_g, L2_conv_bn1_b, L2_conv_bn1_m, L2_conv_bn1_v, L2_conv_woff, L2_conv_boff, L2_conv_w2, L2_conv_dcn_b, L2_conv_bn2_g, L2_conv_bn2_b, L2_conv_bn2_m, L2_conv_bn2_v, L2_conv_w3, L2_conv_bn3_g, L2_conv_bn3_b, L2_conv_bn3_m, L2_conv_bn3_v)
    x = _L3_conv_ref(x, L3_conv_gn1_g, L3_conv_gn1_b, L3_conv_dw1, L3_conv_pw1, L3_conv_pwb1, L3_conv_w1, L3_conv_b1, L3_conv_gn2_g, L3_conv_gn2_b, L3_conv_dw2, L3_conv_pw2, L3_conv_pwb2, L3_conv_w2, L3_conv_b2)
    return x


_drawn_inputs = setup_inputs


def setup_inputs(seed=0):
    import zlib

    import numpy as np

    out = dict(_drawn_inputs(seed))
    spreads = {'L0_conv_gn_gamma': (1.0, 0.2),
     'L0_conv_gn_beta': (0.0, 0.1),
     'L0_conv_b_proj': (0.0, 0.1),
     'L3_conv_gn1_g': (1.0, 0.2),
     'L3_conv_gn1_b': (0.0, 0.1),
     'L3_conv_pwb1': (0.0, 0.1),
     'L3_conv_b1': (0.0, 0.1),
     'L3_conv_gn2_g': (1.0, 0.2),
     'L3_conv_gn2_b': (0.0, 0.1),
     'L3_conv_pwb2': (0.0, 0.1),
     'L3_conv_b2': (0.0, 0.1)}
    factors = {'L2_conv_bn1_b': 13.875,
     'L2_conv_bn1_m': 27.012,
     'L2_conv_bn1_v': 25.464,
     'L2_conv_boff': 17.705,
     'L2_conv_bn2_m': 8.407,
     'L2_conv_bn2_v': 30.517,
     'L2_conv_w1': 3.219,
     'L2_conv_bn1_g': 8.0,
     'L2_conv_woff': 8.0,
     'L2_conv_dcn_b': 3.859,
     'L2_conv_bn2_g': 3.437,
     'L2_conv_bn3_v': 3.097,
     'L2_conv_bn2_b': 4.259}
    for name, (base, spread) in spreads.items():
        noise = np.random.default_rng([zlib.crc32(name.encode()), seed]).standard_normal(out[name].shape)
        drawn = base * np.exp(spread * noise) if base else spread * noise
        out[name] = jnp.asarray(drawn.astype(out[name].dtype))
    for name, factor in factors.items():
        out[name] = (out[name] * factor).astype(out[name].dtype)
    return out
```

```python
from contextlib import ExitStack

import numpy as np

import concourse.bass as bass
from concourse import mybir

F32, F16, I32 = mybir.dt.float32, mybir.dt.float16, mybir.dt.int32
ALU = mybir.AluOpType
ACT = mybir.ActivationFunctionType
AX = mybir.AxisListType

B, C, H, W = 2, 256, 64, 64
PIX = H * W
CH = C // 128
NT = PIX // 128
NHEAD, D = 4, 64
CB = 64
EPS = 1e-5
CHUNK = 512
NCH = PIX // CHUNK
TY = H + 2
KK = 9
PW2, PW7 = W + 2, W + 6
O2, O3 = 27, 18
QK_SCALE, V_SCALE = 16.0, 64.0
LN_P_MAX = 14 * float(np.log(2.0))
NPOS = PIX // C

GN0_G, GN0_B, BN3_G, BN3_B, BN3_M, BN3_V, GN1_G, GN1_B, B1, GN2_G, GN2_B, B2 = range(12)
BN1_G, BN1_B, BN1_M, BN1_V, DCN_B, BN2_G, BN2_B, BN2_M, BN2_V = range(9)


def program(nc, x, wqkv, wproj, pos_l, pos_r, vec, vec64, w1, woff, boff, w2, w3, dw, pw, pwb, wd,
            ident, mean32, mean8, sel2, sel3, base2, base3, out):
    ctx = ExitStack()
    with ctx:
        def sb(name, shape, dt=F32):
            return ctx.enter_context(nc.sbuf_tensor(name, shape, dt))

        def sem(name):
            return ctx.enter_context(nc.semaphore(name))

        attn_dram = nc.dram_tensor("attn_scratch", (PIX, C), F32, kind="Internal").ap()
        table64 = nc.dram_tensor("corners64", (TY * TY, 4 * CB), F32, kind="Internal").ap()
        table256 = nc.dram_tensor("corners256", (TY * TY, 4 * C), F32, kind="Internal").ap()

        X = sb("X", [128, CH, PIX])
        wqkv_s = sb("wqkv_s", [128, CH, 3 * C])
        wproj_s = sb("wproj_s", [128, CH, C])
        pos_r_s = sb("pos_r_s", [6, C])
        vec_s = sb("vec_s", [128, 12, CH])
        vec64_s = sb("vec64_s", [CB, 9])
        w1_s = sb("w1_s", [128, CH, CB])
        woff_s = sb("woff_s", [CB, 3, 3 * O2])
        w2_s = sb("w2_s", [128, 5, CB])
        w3_s = sb("w3_s", [CB, C])
        dw_s = sb("dw_s", [128, 2, CH, 49])
        pw_s = sb("pw_s", [128, 2, CH, O3])
        ident_s = sb("ident_s", [128, 128])
        mean32_s = sb("mean32_s", [128, 128])
        mean8_s = sb("mean8_s", [128, 128])
        sel2_s = sb("sel2_s", [3 * O2, 3, O2])
        sel3_s = sb("sel3_s", [7 * O3, 7, O3])
        boff_s = sb("boff_s", [128, O2])
        pwb_s = sb("pwb_s", [128, 2, O3])
        bnst = sb("bnst", [128, CH, 8, 6])
        mv = sb("mv", [128, CH, 2])
        gm = sb("gm", [128, CH, 2])
        gsq = sb("gsq", [128, CH])
        gvar = sb("gvar", [128, CH])
        grs = sb("grs", [128, CH])
        gsc = sb("gsc", [128, CH])
        gtm = sb("gtm", [128, CH])
        gbi = sb("gbi", [128, CH])
        bn3s = sb("bn3s", [128, CH])
        bn3b = sb("bn3b", [128, CH])
        bnf = sb("bnf", [CB, 8])
        minus_half = sb("minus_half", [128, CH])

        ARENA = 37000
        arena = sb("arena", [128, ARENA])

        class Carver:
            def __init__(self, start=0):
                self.at = start

            def f32(self, *dims, parts=128, dt=F32):
                n = int(np.prod(dims))
                words = n if dt != F16 else n // 2
                view = arena[0:parts, self.at:self.at + words]
                self.at += words
                assert self.at <= ARENA, self.at
                if dt != F32:
                    view = view.bitcast(dt)
                if len(dims) > 1:
                    names = "abcd"[:len(dims)]
                    view = view.rearrange(f"p ({' '.join(names)}) -> p {' '.join(names)}",
                                          **dict(zip(names, dims)))
                return view

        att = Carver()
        QA, QB, KA = (att.f32(PIX, dt=F16) for _ in range(3))
        V = att.f32(NT * NHEAD, 2, D, dt=F16)
        S = [att.f32(PIX) for _ in range(2)]
        P1 = att.f32(4, CHUNK, dt=F16)
        P2 = att.f32(4, CHUNK, dt=F16)
        WQK = att.f32(2, CH, 2, D)
        O1 = [att.f32(2, D) for _ in range(2)]
        AO = [att.f32(D) for _ in range(2)]
        mx = [att.f32(8) for _ in range(2)]
        nmx = [att.f32(1) for _ in range(2)]
        rs = [att.f32(4) for _ in range(2)]
        rsum = [att.f32(1) for _ in range(2)]
        rr = [att.f32(1) for _ in range(2)]
        prj = Carver()
        AOL = [prj.f32(4, C) for _ in range(2)]
        POSL = [prj.f32(2, C, parts=6) for _ in range(2)]
        AT = prj.f32(CH, CHUNK)

        bot = Carver()
        HP2 = bot.f32(PW2 * PW2, parts=CB)
        STG2 = [bot.f32(CHUNK, parts=CB) for _ in range(2)]
        TS2 = [bot.f32(4, CB) for _ in range(2)]
        T2 = bot.f32(8, PW2, parts=3 * O2)
        BASE2 = bot.f32(NT, O2)
        OFF2 = bot.f32(NT, O2)
        MASK2 = bot.f32(NT, KK)
        FR2 = bot.f32(NT, O3)
        FL2 = bot.f32(NT, O3)
        CO2 = bot.f32(NT, O3)
        W4_2 = bot.f32(NT, KK, 4)
        IDX2 = bot.f32(NT, KK, dt=I32)
        G2 = [bot.f32(KK, 4 * CB) for _ in range(2)]
        IS2 = [bot.f32(KK, dt=I32) for _ in range(2)]
        WS2 = [bot.f32(KK * 4) for _ in range(2)]
        A2 = bot.f32(KK, 2 * CB)
        SM2 = [bot.f32(5 * 128) for _ in range(2)]
        SMT2 = [bot.f32(5, 128) for _ in range(2)]
        H2 = [bot.f32(128, parts=CB) for _ in range(2)]

        dcn = Carver()
        OUT = dcn.f32(CH, PIX)
        hole = dcn.at
        HP7 = dcn.f32(CH, PW7 * PW7)
        after = dcn.at
        WD = dcn.f32(KK, CH, C)
        WO = dcn.f32(CH, 7, 7 * O3)
        BASE3 = dcn.f32(NT, O3)
        T3 = dcn.f32(8, PW7, parts=7 * O3)
        OFF3 = dcn.f32(NT, O3)
        FR3 = dcn.f32(NT, O3)
        W4_3 = dcn.f32(NT, KK, 4)
        IDX3 = dcn.f32(NT, KK, dt=I32)
        IS3 = [dcn.f32(4, KK, dt=I32) for _ in range(2)]
        WS3 = [dcn.f32(4 * KK * 4) for _ in range(2)]
        stg = Carver(dcn.at)
        STG3 = [stg.f32(CH, CHUNK) for _ in range(2)]
        TS3 = [stg.f32(4, C) for _ in range(2)]
        SAMP = [dcn.f32(4, C) for _ in range(2)]
        ST = [dcn.f32(CH, CHUNK) for _ in range(2)]
        NG = 8
        ring = Carver(hole)
        G3 = [ring.f32(4, C) for _ in range(NG)]
        assert ring.at <= after
        FO = OUT.rearrange("p a (n c) -> p a n c", c=CHUNK)
        ZERO = Carver().f32(4 * C)

        ps = ctx.enter_context(nc.psum_tensor("ps", [128, 8, CHUNK], F32))
        psf = ps[:, :, :].rearrange("p a b -> p (a b)")

        loaded = sem("loaded")
        dve_step = sem("dve_step")
        act_step = sem("act_step")
        pool_step = sem("pool_step")
        zeroed = sem("zeroed")
        x_loaded = sem("x_loaded")
        gn_stat = sem("gn_stat")
        gn_mean = sem("gn_mean")
        v_ready = sem("v_ready")
        v1_done = sem("v1_done")
        v_free = sem("v_free")
        wqk_ready = sem("wqk_ready")
        q_ready = sem("q_ready")
        k_ready = sem("k_ready")
        q_free = sem("q_free")
        k_free = sem("k_free")
        qa_done = sem("qa_done")
        ka_done = sem("ka_done")
        score_ready = sem("score_ready")
        score_free = sem("score_free")
        row_done = sem("row_done")
        max_ready = sem("max_ready")
        prob_ready = sem("prob_ready")
        tr_ready = sem("tr_ready")
        p1_ready = sem("p1_ready")
        p2_ready = sem("p2_ready")
        rr_ready = sem("rr_ready")
        out_ready = sem("out_ready")
        out_free = sem("out_free")
        o1_ready = sem("o1_ready")
        out_done = sem("out_done")
        ao_free0 = sem("ao_free0")
        ao_free1 = sem("ao_free1")
        aol_ready0 = sem("aol_ready0")
        aol_ready1 = sem("aol_ready1")
        aol_free = sem("aol_free")
        at_ps0 = sem("at_ps0")
        at_ps1 = sem("at_ps1")
        at_ready0 = sem("at_ready0")
        at_ready1 = sem("at_ready1")
        proj_ready = sem("proj_ready")
        proj_free = sem("proj_free")
        h1_ready = sem("h1_ready")
        h1_free = sem("h1_free")
        stage_ready = sem("stage_ready")
        stage_free = sem("stage_free")
        tp_ready = sem("tp_ready")
        tp_free = sem("tp_free")
        ts_ready = sem("ts_ready")
        ts_free0 = sem("ts_free0")
        ts_free1 = sem("ts_free1")
        t_ps = sem("t_ps")
        t_ready = sem("t_ready")
        off_ready = sem("off_ready")
        off_free = sem("off_free")
        mask_in = sem("mask_in")
        mask_ready = sem("mask_ready")
        g2_ready0 = sem("g2_ready0")
        g2_ready1 = sem("g2_ready1")
        g2_free = sem("g2_free")
        sm_ready = sem("sm_ready")
        sm_free = sem("sm_free")
        smt_ps = sem("smt_ps")
        smt_ready = sem("smt_ready")
        d_ready = sem("d_ready")
        h2_ready = sem("h2_ready")
        e_ready = sem("e_ready")
        e_free = sem("e_free")
        g_free = sem("g_free")
        chain = sem("chain")
        samp_ready = sem("samp_ready")
        samp_free = sem("samp_free")
        st_ps = sem("st_ps")
        st_ready = sem("st_ready")
        st_free = sem("st_free")
        o_ready_act = sem("o_ready_act")
        o_ready_dve = sem("o_ready_dve")
        o_free = sem("o_free")
        fo_ready = sem("fo_ready")
        fo_sent = sem("fo_sent")
        wd_loaded = sem("wd_loaded")
        arrived = sem("arrived")
        go_act = sem("go_act")
        go_dve = sem("go_dve")
        go_pe = sem("go_pe")
        go_pool = sem("go_pool")
        scalar_in = sem("scalar_in")
        root_in = sem("root_in")
        root_ready = sem("root_ready")
        gathers_seen = sem("gathers_seen")
        g_ready = [sem(f"g_ready{i}") for i in range(2)]
        ao_free = [ao_free0, ao_free1]
        aol_ready = [aol_ready0, aol_ready1]
        ts_free = [ts_free0, ts_free1]
        g2_ready = [g2_ready0, g2_ready1]

        def chunk(n):
            return bass.ds(n * CHUNK, CHUNK)

        block = ctx.enter_context(nc.Block())

        @block.sync
        def _(sp):
            loads = [(wqkv_s, wqkv), (wproj_s, wproj), (pos_r_s, pos_r), (vec_s, vec), (vec64_s, vec64),
                     (w1_s, w1), (woff_s, woff), (w3_s, w3), (dw_s, dw), (pw_s, pw), (ident_s, ident),
                     (mean32_s, mean32), (mean8_s, mean8), (sel2_s, sel2), (sel3_s, sel3), (boff_s, boff),
                     (pwb_s, pwb)]
            for dst, src in loads:
                sp.dma_start(dst[:], src).then_inc(loaded, 16)
            sp.wait_ge(zeroed, 1)
            sp.sem_inc(zeroed, -1)
            sp.dma_start(w2_s[:, 0:4, :], w2[0:512, :].rearrange("(a p) o -> p a o", p=128)).then_inc(loaded, 16)
            sp.dma_start(w2_s[0:CB, 4, :], w2[512:576, :]).then_inc(loaded, 16)
            n_loads = len(loads) + 2
            for tab, cc in ((table64, CB), (table256, C)):
                rows = tab.rearrange("(y x) c -> y x c", y=TY)
                for yy in (0, H, H + 1):
                    sp.dma_start(tab.rearrange("(y x) c -> y (x c)", y=TY)[yy, :].rearrange("(p f) -> p f", p=128),
                                     ZERO[:, 0:TY * 4 * cc // 128]).then_inc(loaded, 16)
                for xx in (0, W, W + 1):
                    sp.dma_start(rows[1:H, xx, :], ZERO[0:H - 1, 0:4 * cc]).then_inc(loaded, 16)
                n_loads += 6
            sp.wait_ge(loaded, 16 * n_loads)
            sp.sem_inc(loaded, -16 * n_loads)
            sp.drain().then_inc(arrived, 1)
            sp.wait_ge(arrived, 5)
            sp.sem_inc(arrived, -5)
            sp.sem_inc(go_act, 1)
            sp.sem_inc(go_dve, 1)
            sp.sem_inc(go_pe, 1)
            sp.sem_inc(go_pool, 1)

            def table_writes(p, n, stage, table, cc):
                sp.wait_ge(ts_ready, 1)
                sp.sem_inc(ts_ready, -1)
                rows = table.rearrange("(y x) (k c) -> y x k c", y=TY, k=4)
                for dy in range(2):
                    for dx in range(2):
                        for r in range(2):
                            dst = rows[bass.ds(8 * n + r + 1 - dy, 4, 2), 1 - dx:1 - dx + W, 2 * dy + dx, :]
                            sp.dma_start(dst.rearrange("y x c -> x y c"),
                                             stage[r * W:(r + 1) * W, :, :]).then_inc(ts_free[p], 16)

            with sp.Fori(0, B) as b:
                sp.dma_start(X[:, :, :], x[bass.ds(b, 1)].rearrange("o (a p) n -> p (o a) n", p=128)).then_inc(x_loaded, 16)
                sp.drain().then_inc(arrived, 1)
                sp.wait_ge(arrived, 5)
                sp.sem_inc(arrived, -5)
                sp.sem_inc(go_act, 1)
                sp.sem_inc(go_dve, 1)
                sp.sem_inc(go_pe, 1)
                sp.sem_inc(go_pool, 1)
                sp.drain().then_inc(arrived, 1)
                sp.wait_ge(arrived, 5)
                sp.sem_inc(arrived, -5)
                sp.sem_inc(go_act, 1)
                sp.sem_inc(go_dve, 1)
                sp.sem_inc(go_pe, 1)
                sp.sem_inc(go_pool, 1)
                with sp.Fori(0, NHEAD) as h:
                    sp.drain().then_inc(arrived, 1)
                    sp.wait_ge(arrived, 5)
                    sp.sem_inc(arrived, -5)
                    sp.sem_inc(go_act, 1)
                    sp.sem_inc(go_dve, 1)
                    sp.sem_inc(go_pe, 1)
                    sp.sem_inc(go_pool, 1)
                    with sp.Fori(0, NT // 2) as t2:
                        for p in range(2):
                            sp.wait_ge(out_done, 1)
                            sp.sem_inc(out_done, -1)
                            sp.dma_start(attn_dram[bass.ds((2 * t2 + p) * 128, 128), bass.ds(h * D, D)],
                                             AO[p]).then_inc(ao_free[p], 16)
                    for p in range(2):
                        sp.wait_ge(ao_free[p], 16)
                    sp.drain().then_inc(arrived, 1)
                    sp.wait_ge(arrived, 5)
                    sp.sem_inc(arrived, -5)
                    sp.sem_inc(go_act, 1)
                    sp.sem_inc(go_dve, 1)
                    sp.sem_inc(go_pe, 1)
                    sp.sem_inc(go_pool, 1)
                with sp.Fori(0, NCH // 2) as n2:
                    for p in range(2):
                        n = 2 * n2 + p
                        sp.wait_ge(aol_free, 1)
                        sp.sem_inc(aol_free, -1)
                        sp.dma_start(AOL[p], attn_dram[chunk(n), :].rearrange("(a p) c -> p a c", p=128)).then_inc(aol_ready[p], 16)
                        sp.dma_start(POSL[p], pos_l[:, bass.ds(2 * n, 2), :]).then_inc(aol_ready[p], 16)
                sp.drain().then_inc(arrived, 1)
                sp.wait_ge(arrived, 5)
                sp.sem_inc(arrived, -5)
                sp.sem_inc(go_act, 1)
                sp.sem_inc(go_dve, 1)
                sp.sem_inc(go_pe, 1)
                sp.sem_inc(go_pool, 1)
                sp.dma_start(BASE2, base2).then_inc(x_loaded, 16)
                sp.drain().then_inc(arrived, 1)
                sp.wait_ge(arrived, 5)
                sp.sem_inc(arrived, -5)
                sp.sem_inc(go_act, 1)
                sp.sem_inc(go_dve, 1)
                sp.sem_inc(go_pe, 1)
                sp.sem_inc(go_pool, 1)
                with sp.Fori(0, NCH // 2) as n2:
                    for p in range(2):
                        table_writes(p, 2 * n2 + p, TS2[p], table64, CB)
                for p in range(2):
                    sp.wait_ge(ts_free[p], 16 * 8)
                sp.drain().then_inc(arrived, 1)
                sp.wait_ge(arrived, 5)
                sp.sem_inc(arrived, -5)
                sp.sem_inc(go_act, 1)
                sp.sem_inc(go_dve, 1)
                sp.sem_inc(go_pe, 1)
                sp.sem_inc(go_pool, 1)
                sp.drain().then_inc(arrived, 1)
                sp.wait_ge(arrived, 5)
                sp.sem_inc(arrived, -5)
                sp.sem_inc(go_act, 1)
                sp.sem_inc(go_dve, 1)
                sp.sem_inc(go_pe, 1)
                sp.sem_inc(go_pool, 1)
                sp.drain().then_inc(arrived, 1)
                sp.wait_ge(arrived, 5)
                sp.sem_inc(arrived, -5)
                sp.sem_inc(go_act, 1)
                sp.sem_inc(go_dve, 1)
                sp.sem_inc(go_pe, 1)
                sp.sem_inc(go_pool, 1)
                sp.drain().then_inc(arrived, 1)
                sp.wait_ge(arrived, 5)
                sp.sem_inc(arrived, -5)
                sp.sem_inc(go_act, 1)
                sp.sem_inc(go_dve, 1)
                sp.sem_inc(go_pe, 1)
                sp.sem_inc(go_pool, 1)
                sp.drain().then_inc(arrived, 1)
                sp.wait_ge(arrived, 5)
                sp.sem_inc(arrived, -5)
                sp.sem_inc(go_act, 1)
                sp.sem_inc(go_dve, 1)
                sp.sem_inc(go_pe, 1)
                sp.sem_inc(go_pool, 1)
                for layer in range(2):
                    sp.dma_start(WD, wd[layer]).then_inc(wd_loaded, 16)
                    sp.dma_start(BASE3, base3).then_inc(wd_loaded, 16)
                    sp.drain().then_inc(arrived, 1)
                    sp.wait_ge(arrived, 5)
                    sp.sem_inc(arrived, -5)
                    sp.sem_inc(go_act, 1)
                    sp.sem_inc(go_dve, 1)
                    sp.sem_inc(go_pe, 1)
                    sp.sem_inc(go_pool, 1)
                    with sp.Fori(0, NCH // 2) as n2:
                        for p in range(2):
                            table_writes(p, 2 * n2 + p, TS3[p], table256, C)
                    for p in range(2):
                        sp.wait_ge(ts_free[p], 16 * 8)
                    sp.drain().then_inc(arrived, 1)
                    sp.wait_ge(arrived, 5)
                    sp.sem_inc(arrived, -5)
                    sp.sem_inc(go_act, 1)
                    sp.sem_inc(go_dve, 1)
                    sp.sem_inc(go_pe, 1)
                    sp.sem_inc(go_pool, 1)
                    sp.drain().then_inc(arrived, 1)
                    sp.wait_ge(arrived, 5)
                    sp.sem_inc(arrived, -5)
                    sp.sem_inc(go_act, 1)
                    sp.sem_inc(go_dve, 1)
                    sp.sem_inc(go_pe, 1)
                    sp.sem_inc(go_pool, 1)
                    sp.wait_ge(wd_loaded, 32)
                    sp.sem_inc(wd_loaded, -32)
                    sp.drain().then_inc(arrived, 1)
                    sp.wait_ge(arrived, 5)
                    sp.sem_inc(arrived, -5)
                    sp.sem_inc(go_act, 1)
                    sp.sem_inc(go_dve, 1)
                    sp.sem_inc(go_pe, 1)
                    sp.sem_inc(go_pool, 1)
                    if layer == 1:
                        with sp.Fori(0, NCH) as g:
                            for oh in range(CH):
                                sp.wait_ge(fo_ready, 1)
                                sp.sem_inc(fo_ready, -1)
                                sp.dma_start(out[bass.ds(b, 1), oh * 128:(oh + 1) * 128, chunk(g)]
                                                 .rearrange("o p n -> p (o n)"), OUT[:, oh, chunk(g)]).then_inc(fo_sent, 16)
                        sp.wait_ge(fo_sent, 16 * NCH * CH)
                        sp.sem_inc(fo_sent, -16 * NCH * CH)
                    sp.drain().then_inc(arrived, 1)
                    sp.wait_ge(arrived, 5)
                    sp.sem_inc(arrived, -5)
                    sp.sem_inc(go_act, 1)
                    sp.sem_inc(go_dve, 1)
                    sp.sem_inc(go_pe, 1)
                    sp.sem_inc(go_pool, 1)

        @block.gpsimd
        def _(pool):
            pool.memset(w2_s[:, 4, :], 0.0).then_inc(pool_step, 1)
            pool.wait_ge(pool_step, 1)
            pool.sem_inc(pool_step, -1)
            pool.memset(minus_half[:, :], -0.5).then_inc(pool_step, 1)
            pool.wait_ge(pool_step, 1)
            pool.sem_inc(pool_step, -1)
            pool.memset(ZERO, 0.0).then_inc(pool_step, 1)
            pool.wait_ge(pool_step, 1)
            pool.sem_inc(pool_step, -1)
            pool.sem_inc(zeroed, 1)
            pool.drain().then_inc(arrived, 1)
            pool.wait_ge(go_pool, 1)
            pool.sem_inc(go_pool, -1)

            def inverse_root(ap):
                pool.wait_ge(root_in, 1)
                pool.sem_inc(root_in, -1)
                pool.tensor_tensor(ap, ap, minus_half[0:ap.shape[0], 0:ap.shape[1]], ALU.pow).then_inc(root_ready, 1)

            inverse_root(bnf[:, 0:1])
            inverse_root(bnf[:, 2:3])
            inverse_root(bn3s[:, :])
            with pool.Fori(0, B) as b:
                inverse_root(grs[:, :])
                pool.drain().then_inc(arrived, 1)
                pool.wait_ge(go_pool, 1)
                pool.sem_inc(go_pool, -1)
                pool.drain().then_inc(arrived, 1)
                pool.wait_ge(go_pool, 1)
                pool.sem_inc(go_pool, -1)
                with pool.Fori(0, NHEAD) as h:
                    for qk in range(2):
                        for dup in range(2):
                            pool.tensor_copy(WQK[:, qk, :, dup, :], wqkv_s[:, :, bass.ds(qk * C + h * D, D)]).then_inc(wqk_ready, 1)
                    pool.drain().then_inc(arrived, 1)
                    pool.wait_ge(go_pool, 1)
                    pool.sem_inc(go_pool, -1)
                    with pool.Fori(0, NT // 2) as t2:
                        for p in range(2):
                            pool.wait_ge(o1_ready, 1)
                            pool.sem_inc(o1_ready, -1)
                            pool.wait_ge(ao_free[p], 16)
                            pool.sem_inc(ao_free[p], -16)
                            pool.tensor_tensor(AO[p], O1[p][:, 0, :], O1[p][:, 1, :], ALU.add).then_inc(pool_step, 1)
                            pool.wait_ge(pool_step, 1)
                            pool.sem_inc(pool_step, -1)
                            pool.sem_inc(out_free, 1)
                            pool.tensor_scalar(AO[p], AO[p], 1.0 / V_SCALE, None, ALU.mult).then_inc(out_done, 1)
                    pool.drain().then_inc(arrived, 1)
                    pool.wait_ge(go_pool, 1)
                    pool.sem_inc(go_pool, -1)
                pool.drain().then_inc(arrived, 1)
                pool.wait_ge(go_pool, 1)
                pool.sem_inc(go_pool, -1)
                pool.memset(HP2, 0.0).then_inc(pool_step, 1)
                pool.wait_ge(pool_step, 1)
                pool.sem_inc(pool_step, -1)
                for p in range(2):
                    pool.memset(SM2[p], 0.0).then_inc(pool_step, 1)
                    pool.wait_ge(pool_step, 1)
                    pool.sem_inc(pool_step, -1)
                pool.drain().then_inc(arrived, 1)
                pool.wait_ge(go_pool, 1)
                pool.sem_inc(go_pool, -1)
                pool.drain().then_inc(arrived, 1)
                pool.wait_ge(go_pool, 1)
                pool.sem_inc(go_pool, -1)
                pool.drain().then_inc(arrived, 1)
                pool.wait_ge(go_pool, 1)
                pool.sem_inc(go_pool, -1)
                pool.drain().then_inc(arrived, 1)
                pool.wait_ge(go_pool, 1)
                pool.sem_inc(go_pool, -1)
                with pool.Fori(0, NT // 2) as t2:
                    for p in range(2):
                        pool.wait_ge(g2_free, 1)
                        pool.sem_inc(g2_free, -1)
                        pool.tensor_copy(IS2[p], IDX2[:, bass.ds(2 * t2 + p, 1), :]
                                                                 .rearrange("p a k -> p (a k)")).then_inc(pool_step, 1)
                        pool.wait_ge(pool_step, 1)
                        pool.sem_inc(pool_step, -1)
                        for k in range(KK):
                            pool.indirect_dma_start(G2[p][:, k, :], None, table64,
                                                        bass.IndirectOffsetOnAxis(ap=IS2[p][:, k:k + 1], axis=0)).then_inc(g2_ready[p], 16)
                pool.drain().then_inc(arrived, 1)
                pool.wait_ge(go_pool, 1)
                pool.sem_inc(go_pool, -1)
                pool.drain().then_inc(arrived, 1)
                pool.wait_ge(go_pool, 1)
                pool.sem_inc(go_pool, -1)
                for layer in range(2):
                    pool.memset(HP7.rearrange("p a n -> p (a n)"), 0.0).then_inc(pool_step, 1)
                    pool.wait_ge(pool_step, 1)
                    pool.sem_inc(pool_step, -1)
                    inverse_root(grs[:, :])
                    pool.drain().then_inc(arrived, 1)
                    pool.wait_ge(go_pool, 1)
                    pool.sem_inc(go_pool, -1)
                    pool.drain().then_inc(arrived, 1)
                    pool.wait_ge(go_pool, 1)
                    pool.sem_inc(go_pool, -1)
                    pool.drain().then_inc(arrived, 1)
                    pool.wait_ge(go_pool, 1)
                    pool.sem_inc(go_pool, -1)
                    pool.drain().then_inc(arrived, 1)
                    pool.wait_ge(go_pool, 1)
                    pool.sem_inc(go_pool, -1)
                    with pool.Fori(0, NCH // 2) as g2:
                        for p in range(2):
                            pool.tensor_copy(
                                IS3[p].rearrange("p a k -> p (a k)"),
                                IDX3.rearrange("p a k -> p (a k)")[:, bass.ds((2 * g2 + p) * 4 * KK, 4 * KK)]).then_inc(pool_step, 1)
                            pool.wait_ge(pool_step, 1)
                            pool.sem_inc(pool_step, -1)
                            for k in range(KK):
                                for t in range(4):
                                    par = (KK * p + k) % 2
                                    slot = 4 * par + t
                                    pool.wait_ge(g_free, 1)
                                    pool.sem_inc(g_free, -1)
                                    pool.indirect_dma_start(
                                        G3[slot].rearrange("p a c -> p (a c)"), None, table256,
                                        bass.IndirectOffsetOnAxis(ap=IS3[p][:, t, k:k + 1], axis=0)).then_inc(g_ready[par], 16)
                    pool.drain().then_inc(arrived, 1)
                    pool.wait_ge(go_pool, 1)
                    pool.sem_inc(go_pool, -1)

        @block.tensor
        def _(pe):
            mm, tr = nc.tensor.matmul, nc.tensor.transpose
            pe.drain().then_inc(arrived, 1)
            pe.wait_ge(go_pe, 1)
            pe.sem_inc(go_pe, -1)

            def gn_means(groups):
                pe.wait_ge(gn_stat, 1)
                pe.sem_inc(gn_stat, -1)
                mm(ps[:, 7, 0:2 * CH], groups[:, :], mv[:, :, :].rearrange("p a b -> p (a b)"),
                       start=True, stop=True).then_inc(gn_mean, 1)

            def offset_conv(img, halves, pw_, ksize, wts, tbuf, no, sel):
                ko = ksize * no
                n = 4 * pw_
                with pe.Fori(0, NCH) as blk:
                    for j in range(2):
                        first = True
                        for half in range(halves):
                            for ky in range(ksize):
                                last = mm(ps[0:ko, j, 0:n], wts(half, ky),
                                          img(half)[:, bass.ds((8 * blk + 4 * j + ky) * pw_, n)],
                                          start=first, stop=(half == halves - 1 and ky == ksize - 1))
                                first = False
                        last.then_inc(t_ps, 1)
                    pe.wait_ge(t_ready, 2)
                    pe.sem_inc(t_ready, -2)
                    pe.wait_ge(off_free, 1)
                    pe.sem_inc(off_free, -1)
                    for t in range(4):
                        for kx in range(ksize):
                            for r in range(2):
                                last = mm(ps[r * W:(r + 1) * W, 2, t * no:(t + 1) * no],
                                          tbuf[:, 2 * t + r, kx:kx + W], sel[:, kx, :],
                                          start=(kx == 0), stop=(kx == ksize - 1))
                    last.then_inc(off_ready, 1)

            with pe.Fori(0, B) as b:
                gn_means(mean32_s)
                pe.drain().then_inc(arrived, 1)
                pe.wait_ge(go_pe, 1)
                pe.sem_inc(go_pe, -1)
                for j in range(NT // 2):
                    pe.wait_ge(v_free, 1)
                    pe.sem_inc(v_free, -1)
                    for k in range(2):
                        for half in range(CH):
                            t = 2 * j + k
                            last = mm(ps[:, j % 4, k * C:(k + 1) * C], X[:, half, t * 128:(t + 1) * 128],
                                      wqkv_s[:, half, 2 * C:3 * C], start=(half == 0), stop=(half == CH - 1))
                    last.then_inc(v_ready, 1)
                pe.drain().then_inc(arrived, 1)
                pe.wait_ge(go_pe, 1)
                pe.sem_inc(go_pe, -1)
                with pe.Fori(0, NHEAD) as h:
                    pe.wait_ge(wqk_ready, 4)
                    pe.sem_inc(wqk_ready, -4)
                    with pe.Fori(0, NCH // 2) as n2:
                        for p in range(2):
                            for qk in range(2):
                                pe.wait_ge((q_free, k_free)[qk], 1)
                                pe.sem_inc((q_free, k_free)[qk], -1)
                                for half in range(CH):
                                    last = mm(ps[:, 2 * p + qk, :],
                                              WQK[:, qk, half, :, :].rearrange("p a b -> p (a b)"),
                                              X[:, half, chunk(2 * n2 + p)],
                                              start=(half == 0), stop=(half == CH - 1))
                                last.then_inc((q_ready, k_ready)[qk], 1)
                    pe.drain().then_inc(arrived, 1)
                    pe.wait_ge(go_pe, 1)
                    pe.sem_inc(go_pe, -1)

                    def score_tile(t, g):
                        pe.wait_ge(score_free, 1)
                        pe.sem_inc(score_free, -1)
                        for q, qs in enumerate((QA, QB)):
                            last = mm(ps[:, g % 2, :], qs[:, bass.ds(t * 128, 128)],
                                      KA[:, g * CHUNK:(g + 1) * CHUNK], start=(q == 0), stop=(q == 1))
                        last.then_inc(score_ready, 1)

                    def values(p, g):
                        if g == 0:
                            pe.wait_ge(out_free, 1)
                            pe.sem_inc(out_free, -1)
                        pe.wait_ge(p2_ready, 1)
                        pe.sem_inc(p2_ready, -1)
                        for k in range(4):
                            j = 4 * g + k
                            for q, part in enumerate((P1, P2)):
                                last = mm(ps[:, 6 + p, 0:2 * D], part[:, g % 4, k * 128:(k + 1) * 128],
                                          V[:, bass.ds(j * NHEAD + h, 1), :, :].rearrange("p o a d -> p (o a d)"),
                                          start=(j == 0 and q == 0), stop=(j == NT - 1 and q == 1))
                        if g == 7:
                            last.then_inc(out_ready, 1)

                    def slot(p, before=True, ahead=None):
                        for g in range(8):
                            if g % 2 == 0:
                                pe.wait_ge(prob_ready, 1)
                                pe.sem_inc(prob_ready, -1)
                            for k in range(4):
                                last = tr(ps[:, 2 + g % 4, k * 128:(k + 1) * 128],
                                          S[p][:, (4 * g + k) * 128:(4 * g + k + 1) * 128], ident_s[:, :])
                            last.then_inc(tr_ready, 1)
                            if ahead is not None:
                                score_tile(ahead, g)
                            if g >= 2:
                                values(p, g - 2)
                            elif before:
                                values(1 - p, g + 6)

                    for t in range(2):
                        for g in range(8):
                            score_tile(t, g)
                    slot(0, before=False, ahead=2)
                    with pe.Fori(0, NT // 2 - 2) as t2:
                        slot(1, ahead=2 * t2 + 3)
                        slot(0, ahead=2 * t2 + 4)
                    slot(1, ahead=NT - 1)
                    slot(0)
                    slot(1)
                    values(1, 6)
                    values(1, 7)
                    pe.drain().then_inc(arrived, 1)
                    pe.wait_ge(go_pe, 1)
                    pe.sem_inc(go_pe, -1)
                with pe.Fori(0, NCH // 2) as n2:
                    for p in range(2):
                        pe.wait_ge(aol_ready[p], 32)
                        pe.sem_inc(aol_ready[p], -32)
                        for half in range(CH):
                            for t in range(4):
                                last = tr(ps[:, half, t * 128:(t + 1) * 128],
                                          AOL[p][:, t, half * 128:(half + 1) * 128], ident_s[:, :])
                            last.then_inc((at_ps0, at_ps1)[half], 1)
                        pe.wait_ge(at_ready0, 1)
                        pe.sem_inc(at_ready0, -1)
                        pe.wait_ge(at_ready1, 1)
                        pe.sem_inc(at_ready1, -1)
                        for oh in range(CH):
                            pe.wait_ge(proj_free, 1)
                            pe.sem_inc(proj_free, -1)
                            for half in range(CH):
                                mm(ps[:, 2 + oh, :], wproj_s[:, half, oh * 128:(oh + 1) * 128], AT[:, half, :],
                                   start=(half == 0), stop=False)
                            for k in range(2):
                                last = mm(ps[:, 2 + oh, k * C:(k + 1) * C], POSL[p][:, k, oh * 128:(oh + 1) * 128],
                                          pos_r_s[:, :], start=False, stop=(k == 1))
                            last.then_inc(proj_ready, 1)
                pe.drain().then_inc(arrived, 1)
                pe.wait_ge(go_pe, 1)
                pe.sem_inc(go_pe, -1)
                pe.drain().then_inc(arrived, 1)
                pe.wait_ge(go_pe, 1)
                pe.sem_inc(go_pe, -1)
                with pe.Fori(0, NCH // 2) as n2:
                    for p in range(2):
                        pe.wait_ge(h1_free, 1)
                        pe.sem_inc(h1_free, -1)
                        for half in range(CH):
                            last = mm(ps[0:CB, p, :], w1_s[:, half, :], X[:, half, chunk(2 * n2 + p)],
                                      start=(half == 0), stop=(half == CH - 1))
                        last.then_inc(h1_ready, 1)
                        pe.wait_ge(stage_ready, 1)
                        pe.sem_inc(stage_ready, -1)
                        pe.wait_ge(tp_free, 1)
                        pe.sem_inc(tp_free, -1)
                        for t in range(4):
                            last = tr(ps[:, 2, t * CB:(t + 1) * CB], STG2[p][:, t * 128:(t + 1) * 128],
                                      ident_s[0:CB, 0:CB])
                        last.then_inc(tp_ready, 1)
                pe.drain().then_inc(arrived, 1)
                pe.wait_ge(go_pe, 1)
                pe.sem_inc(go_pe, -1)
                offset_conv(lambda half: HP2, 1, PW2, 3, lambda half, ky: woff_s[:, ky, :], T2, O2, sel2_s)
                pe.drain().then_inc(arrived, 1)
                pe.wait_ge(go_pe, 1)
                pe.sem_inc(go_pe, -1)
                pe.drain().then_inc(arrived, 1)
                pe.wait_ge(go_pe, 1)
                pe.sem_inc(go_pe, -1)
                with pe.Fori(0, NT // 2) as t2:
                    for p in range(2):
                        pe.wait_ge(sm_ready, 1)
                        pe.sem_inc(sm_ready, -1)
                        for i in range(5):
                            last = tr(psf[:, i * 128:(i + 1) * 128], SM2[p][:, i * 128:(i + 1) * 128],
                                      ident_s[:, :])
                        last.then_inc(smt_ps, 1)
                        pe.wait_ge(smt_ready, 1)
                        pe.sem_inc(smt_ready, -1)
                        for i in range(5):
                            last = mm(ps[0:CB, 2, 0:128], w2_s[:, i, :], SMT2[p][:, i, :],
                                      start=(i == 0), stop=(i == 4))
                        last.then_inc(d_ready, 1)
                        pe.wait_ge(h2_ready, 1)
                        pe.sem_inc(h2_ready, -1)
                        pe.wait_ge(e_free, 1)
                        pe.sem_inc(e_free, -1)
                        for oh in range(CH):
                            last = mm(ps[:, 3 + p, oh * 128:(oh + 1) * 128], w3_s[:, oh * 128:(oh + 1) * 128],
                                      H2[p], start=True, stop=True)
                        last.then_inc(e_ready, 1)
                pe.drain().then_inc(arrived, 1)
                pe.wait_ge(go_pe, 1)
                pe.sem_inc(go_pe, -1)
                pe.drain().then_inc(arrived, 1)
                pe.wait_ge(go_pe, 1)
                pe.sem_inc(go_pe, -1)
                for layer in range(2):
                    gn_means(mean8_s)
                    pe.drain().then_inc(arrived, 1)
                    pe.wait_ge(go_pe, 1)
                    pe.sem_inc(go_pe, -1)
                    with pe.Fori(0, NCH // 2) as n2:
                        for p in range(2):
                            pe.wait_ge(stage_ready, 2)
                            pe.sem_inc(stage_ready, -2)
                            pe.wait_ge(tp_free, 1)
                            pe.sem_inc(tp_free, -1)
                            for t in range(4):
                                for half in range(CH):
                                    last = tr(psf[:, t * C + half * 128:t * C + (half + 1) * 128],
                                              STG3[p][:, half, t * 128:(t + 1) * 128], ident_s[:, :])
                            last.then_inc(tp_ready, 1)
                    pe.drain().then_inc(arrived, 1)
                    pe.wait_ge(go_pe, 1)
                    pe.sem_inc(go_pe, -1)
                    offset_conv(lambda half: HP7[:, half, :], CH, PW7, 7, lambda half, ky: WO[:, half, ky, :],
                                T3, O3, sel3_s)
                    pe.drain().then_inc(arrived, 1)
                    pe.wait_ge(go_pe, 1)
                    pe.sem_inc(go_pe, -1)
                    pe.drain().then_inc(arrived, 1)
                    pe.wait_ge(go_pe, 1)
                    pe.sem_inc(go_pe, -1)
                    with pe.Fori(0, NCH // 2) as g2:
                        for p in range(2):
                            pe.wait_ge(o_free, 2)
                            pe.sem_inc(o_free, -2)

                            def tap(k):
                                par = (KK * p + k) % 2
                                pe.wait_ge(st_ready, CH)
                                pe.sem_inc(st_ready, -CH)
                                for oh in range(CH):
                                    for half in range(CH):
                                        last = mm(ps[:, 4 + 2 * p + oh, :],
                                                  WD[:, k, half, oh * 128:(oh + 1) * 128], ST[par][:, half, :],
                                                  start=(k == 0 and half == 0), stop=(k == KK - 1 and half == CH - 1))
                                    if k == KK - 1:
                                        last.then_inc(o_ready_dve if layer else o_ready_act, 1)
                                if k < KK - 1:
                                    last.then_inc(st_free, 1)

                            for k in range(KK):
                                par = (KK * p + k) % 2
                                for half in range(CH):
                                    for t in range(4):
                                        if half == 0:
                                            pe.wait_ge(samp_ready, 1)
                                            pe.sem_inc(samp_ready, -1)
                                            pe.sem_inc(g_free, 1)
                                        last = tr(ps[:, 2 * par + half, t * 128:(t + 1) * 128],
                                                  SAMP[par][:, t, half * 128:(half + 1) * 128], ident_s[:, :])
                                    last.then_inc(st_ps, 1)
                                if k > 0:
                                    tap(k - 1)
                            tap(KK - 1)
                    pe.drain().then_inc(arrived, 1)
                    pe.wait_ge(go_pe, 1)
                    pe.sem_inc(go_pe, -1)

        @block.scalar
        def _(act):
            af = nc.scalar.activation
            act.drain().then_inc(arrived, 1)
            act.wait_ge(go_act, 1)
            act.sem_inc(go_act, -1)

            def offsets_out(ksize, pw_, tbuf, no):
                n = 4 * pw_
                with act.Fori(0, NCH) as blk:
                    for j in range(2):
                        act.wait_ge(t_ps, 1)
                        act.sem_inc(t_ps, -1)
                        af(tbuf[:, 4 * j:4 * j + 4, :].rearrange("p a b -> p (a b)"),
                               ps[0:ksize * no, j, 0:n], ACT.Copy).then_inc(t_ready, 1)

            with act.Fori(0, B) as b:
                act.wait_ge(scalar_in, 1)
                act.sem_inc(scalar_in, -1)
                af(X[:, 1, :], X[:, 1, :], ACT.Identity, scale=gsc[:, 1:2], bias=gbi[:, 1:2]).then_inc(act_step, 1)
                act.wait_ge(act_step, 1)
                act.sem_inc(act_step, -1)
                act.drain().then_inc(arrived, 1)
                act.wait_ge(go_act, 1)
                act.sem_inc(go_act, -1)
                for j in range(NT // 2):
                    act.wait_ge(v_ready, 1)
                    act.sem_inc(v_ready, -1)
                    af(V[:, 2 * j * NHEAD:2 * (j + 1) * NHEAD, 0, :],
                           ps[:, j % 4, :].rearrange("p (a d) -> p a d", d=D), ACT.Copy, scale=V_SCALE).then_inc(v1_done, 1)
                act.drain().then_inc(arrived, 1)
                act.wait_ge(go_act, 1)
                act.sem_inc(go_act, -1)
                with act.Fori(0, NHEAD) as h:
                    with act.Fori(0, NCH // 2) as n2:
                        for p in range(2):
                            n = 2 * n2 + p
                            act.wait_ge(q_ready, 1)
                            act.sem_inc(q_ready, -1)
                            af(QA[:, chunk(n)], ps[:, 2 * p, :], ACT.Copy, scale=QK_SCALE).then_inc(qa_done, 1)
                            act.wait_ge(k_ready, 1)
                            act.sem_inc(k_ready, -1)
                            af(KA[:, chunk(n)], ps[:, 2 * p + 1, :], ACT.Copy, scale=QK_SCALE).then_inc(ka_done, 1)
                    act.drain().then_inc(arrived, 1)
                    act.wait_ge(go_act, 1)
                    act.sem_inc(go_act, -1)

                    def softmax(p, i):
                        if i == 0:
                            act.wait_ge(max_ready, 1)
                            act.sem_inc(max_ready, -1)
                        at = slice(i * 1024, (i + 1) * 1024)
                        af(S[p][:, at], S[p][:, at], ACT.Exp, bias=nmx[p], accum_out=rs[p][:, i:i + 1]).then_inc(prob_ready, 1)

                    def slot(p, before=True, ahead=True):
                        for g in range(8):
                            act.wait_ge(tr_ready, 1)
                            act.sem_inc(tr_ready, -1)
                            af(P1[:, g % 4, :], ps[:, 2 + g % 4, :], ACT.Copy).then_inc(p1_ready, 1)
                            if ahead and g % 2 == 0:
                                softmax(1 - p, g // 2)
                            if before and g == 3:
                                output(1 - p)

                    def output(p):
                        act.wait_ge(rr_ready, 1)
                        act.sem_inc(rr_ready, -1)
                        act.wait_ge(out_ready, 1)
                        act.sem_inc(out_ready, -1)
                        af(O1[p].rearrange("p a d -> p (a d)"), ps[:, 6 + p, 0:2 * D], ACT.Copy, scale=rr[p]).then_inc(o1_ready, 1)

                    for i in range(4):
                        softmax(0, i)
                    slot(0, before=False)
                    with act.Fori(0, NT // 2 - 1) as t2:
                        slot(1)
                        slot(0)
                    slot(1, ahead=False)
                    output(1)
                    act.drain().then_inc(arrived, 1)
                    act.wait_ge(go_act, 1)
                    act.sem_inc(go_act, -1)
                with act.Fori(0, NCH // 2) as n2:
                    for p in range(2):
                        act.wait_ge(at_ps1, 1)
                        act.sem_inc(at_ps1, -1)
                        af(AT[:, 1, :], ps[:, 1, :], ACT.Copy).then_inc(at_ready1, 1)
                act.drain().then_inc(arrived, 1)
                act.wait_ge(go_act, 1)
                act.sem_inc(go_act, -1)
                act.drain().then_inc(arrived, 1)
                act.wait_ge(go_act, 1)
                act.sem_inc(go_act, -1)
                with act.Fori(0, NCH // 2) as n2:
                    for p in range(2):
                        n = 2 * n2 + p
                        act.wait_ge(h1_ready, 1)
                        act.sem_inc(h1_ready, -1)
                        act.wait_ge(stage_free, 1)
                        act.sem_inc(stage_free, -1)
                        af(STG2[p], ps[0:CB, p, :], ACT.Relu, scale=bnf[:, 0:1], bias=bnf[:, 1:2]).then_inc(stage_ready, 1)
                        af(HP2.rearrange("p (y x) -> p y x", y=PW2)[:, bass.ds(8 * n + 1, 8), 1:1 + W],
                               ps[0:CB, p, :].rearrange("p (y x) -> p y x", x=W), ACT.Relu,
                               scale=bnf[:, 0:1], bias=bnf[:, 1:2]).then_inc(h1_free, 1)
                act.drain().then_inc(arrived, 1)
                act.wait_ge(go_act, 1)
                act.sem_inc(go_act, -1)
                offsets_out(3, PW2, T2, O2)
                act.drain().then_inc(arrived, 1)
                act.wait_ge(go_act, 1)
                act.sem_inc(go_act, -1)
                af(MASK2, OFF2[:, :, O3:O2], ACT.Sigmoid).then_inc(mask_ready, 1)
                act.drain().then_inc(arrived, 1)
                act.wait_ge(go_act, 1)
                act.sem_inc(go_act, -1)
                with act.Fori(0, NT // 2) as t2:
                    for p in range(2):
                        act.wait_ge(smt_ps, 1)
                        act.sem_inc(smt_ps, -1)
                        act.sem_inc(sm_free, 1)
                        af(SMT2[p].rearrange("p a b -> p (a b)"), psf[:, 0:5 * 128], ACT.Copy).then_inc(smt_ready, 1)
                        act.wait_ge(d_ready, 1)
                        act.sem_inc(d_ready, -1)
                        af(H2[p], ps[0:CB, 2, 0:128], ACT.Relu, scale=bnf[:, 2:3], bias=bnf[:, 3:4]).then_inc(h2_ready, 1)
                act.drain().then_inc(arrived, 1)
                act.wait_ge(go_act, 1)
                act.sem_inc(go_act, -1)
                af(X[:, 0, :], X[:, 0, :], ACT.Relu, bias=bn3b[:, 0:1]).then_inc(act_step, 1)
                act.wait_ge(act_step, 1)
                act.sem_inc(act_step, -1)
                act.drain().then_inc(arrived, 1)
                act.wait_ge(go_act, 1)
                act.sem_inc(go_act, -1)
                for layer in range(2):
                    src = X[:, :, :] if layer == 0 else OUT
                    act.drain().then_inc(arrived, 1)
                    act.wait_ge(go_act, 1)
                    act.sem_inc(go_act, -1)
                    with act.Fori(0, NCH // 2) as n2:
                        for p in range(2):
                            n = 2 * n2 + p
                            act.wait_ge(stage_free, 1)
                            act.sem_inc(stage_free, -1)
                            for half in range(CH):
                                af(STG3[p][:, half, :], src[:, half, chunk(n)], ACT.Relu,
                                       scale=gsc[:, half:half + 1], bias=gbi[:, half:half + 1]).then_inc(stage_ready, 1)
                            for half in range(CH):
                                padded = HP7[:, half, :].rearrange("p (y x) -> p y x", y=PW7)
                                af(padded[:, bass.ds(8 * n + 3, 8), 3:3 + W],
                                       src[:, half, chunk(n)].rearrange("p (y x) -> p y x", x=W), ACT.Relu,
                                       scale=gsc[:, half:half + 1], bias=gbi[:, half:half + 1]).then_inc(act_step, 1)
                            act.wait_ge(act_step, 2)
                            act.sem_inc(act_step, -2)
                    act.drain().then_inc(arrived, 1)
                    act.wait_ge(go_act, 1)
                    act.sem_inc(go_act, -1)
                    offsets_out(7, PW7, T3, O3)
                    act.drain().then_inc(arrived, 1)
                    act.wait_ge(go_act, 1)
                    act.sem_inc(go_act, -1)
                    act.drain().then_inc(arrived, 1)
                    act.wait_ge(go_act, 1)
                    act.sem_inc(go_act, -1)
                    with act.Fori(0, NCH // 2) as g2:
                        for p in range(2):
                            for k in range(KK):
                                par = (KK * p + k) % 2
                                act.wait_ge(st_free, 1)
                                act.sem_inc(st_free, -1)
                                for half in range(CH):
                                    act.wait_ge(st_ps, 1)
                                    act.sem_inc(st_ps, -1)
                                    if half == CH - 1:
                                        act.sem_inc(samp_free, 1)
                                    af(ST[par][:, half, :], ps[:, 2 * par + half, :], ACT.Copy).then_inc(st_ready, 1)
                            if layer == 0:
                                for oh in range(CH):
                                    act.wait_ge(o_ready_act, 1)
                                    act.sem_inc(o_ready_act, -1)
                                    if oh == CH - 1:
                                        act.sem_inc(st_free, 1)
                                    af(OUT[:, oh, chunk(2 * g2 + p)], ps[:, 4 + 2 * p + oh, :], ACT.Identity,
                                           bias=vec_s[:, B1, oh:oh + 1]).then_inc(o_free, 1)
                    act.drain().then_inc(arrived, 1)
                    act.wait_ge(go_act, 1)
                    act.sem_inc(go_act, -1)

        @block.vector
        def _(dve):
            v = nc.vector
            dve.sem_inc(v_free, 4)
            dve.sem_inc(q_free, 2)
            dve.sem_inc(k_free, 2)
            dve.sem_inc(score_free, 2)
            dve.sem_inc(out_free, 2)
            dve.sem_inc(ao_free0, 16)
            dve.sem_inc(ao_free1, 16)
            dve.sem_inc(aol_free, 2)
            dve.sem_inc(proj_free, 2)
            dve.sem_inc(h1_free, 2)
            dve.sem_inc(stage_free, 2)
            dve.sem_inc(tp_free, 1)
            dve.sem_inc(ts_free0, 128)
            dve.sem_inc(ts_free1, 128)
            dve.sem_inc(off_free, 1)
            dve.sem_inc(g2_free, 2)
            dve.sem_inc(sm_free, 2)
            dve.sem_inc(e_free, 2)
            dve.sem_inc(g_free, NG)
            dve.sem_inc(samp_free, 2)
            dve.sem_inc(st_free, 2)
            dve.sem_inc(o_free, 4)
            dve.drain().then_inc(arrived, 1)
            dve.wait_ge(go_dve, 1)
            dve.sem_inc(go_dve, -1)


            def fold(sc, bi, g, bb, m, var, extra=None):
                v.tensor_scalar(sc, var, EPS, None, ALU.add).then_inc(dve_step, 1)
                dve.wait_ge(dve_step, 1)
                dve.sem_inc(dve_step, -1)
                dve.sem_inc(root_in, 1)
                dve.wait_ge(root_ready, 1)
                dve.sem_inc(root_ready, -1)
                v.tensor_tensor(sc, sc, g, ALU.mult).then_inc(dve_step, 1)
                dve.wait_ge(dve_step, 1)
                dve.sem_inc(dve_step, -1)
                if extra is None:
                    v.tensor_tensor(bi, m, sc, ALU.mult).then_inc(dve_step, 1)
                    dve.wait_ge(dve_step, 1)
                    dve.sem_inc(dve_step, -1)
                    v.tensor_tensor(bi, bb, bi, ALU.subtract).then_inc(dve_step, 1)
                    dve.wait_ge(dve_step, 1)
                    dve.sem_inc(dve_step, -1)
                else:
                    v.tensor_tensor(bi, extra, m, ALU.subtract).then_inc(dve_step, 1)
                    dve.wait_ge(dve_step, 1)
                    dve.sem_inc(dve_step, -1)
                    v.tensor_tensor(bi, bi, sc, ALU.mult).then_inc(dve_step, 1)
                    dve.wait_ge(dve_step, 1)
                    dve.sem_inc(dve_step, -1)
                    v.tensor_tensor(bi, bi, bb, ALU.add).then_inc(dve_step, 1)
                    dve.wait_ge(dve_step, 1)
                    dve.sem_inc(dve_step, -1)

            def col(i):
                return vec64_s[:, i:i + 1]
            fold(bnf[:, 0:1], bnf[:, 1:2], col(BN1_G), col(BN1_B), col(BN1_M), col(BN1_V))
            fold(bnf[:, 2:3], bnf[:, 3:4], col(BN2_G), col(BN2_B), col(BN2_M), col(BN2_V), col(DCN_B))
            fold(bn3s[:, :], bn3b[:, :], vec_s[:, BN3_G, :], vec_s[:, BN3_B, :], vec_s[:, BN3_M, :],
                 vec_s[:, BN3_V, :])

            def group_norm(src, gamma, beta):
                for half in range(CH):
                    for c in range(8):
                        last = v.bn_stats(bnst[:, half, c, :], src[:, half, c * 512:(c + 1) * 512])
                last.then_inc(dve_step, 1)
                dve.wait_ge(dve_step, 1)
                dve.sem_inc(dve_step, -1)
                for half in range(CH):
                    last = v.bn_aggr(mv[:, half, :], bnst[:, half, :, :].rearrange("p a b -> p (a b)"))
                last.then_inc(dve_step, 1)
                dve.wait_ge(dve_step, 1)
                dve.sem_inc(dve_step, -1)
                v.tensor_tensor(gsq[:, :], mv[:, :, 0], mv[:, :, 0], ALU.mult).then_inc(dve_step, 1)
                dve.wait_ge(dve_step, 1)
                dve.sem_inc(dve_step, -1)
                v.tensor_tensor(mv[:, :, 1], mv[:, :, 1], gsq[:, :], ALU.add).then_inc(dve_step, 1)
                dve.wait_ge(dve_step, 1)
                dve.sem_inc(dve_step, -1)
                dve.sem_inc(gn_stat, 1)
                dve.wait_ge(gn_mean, 1)
                dve.sem_inc(gn_mean, -1)
                v.tensor_copy(gm[:, :, :].rearrange("p a b -> p (a b)"), ps[:, 7, 0:2 * CH]).then_inc(dve_step, 1)
                dve.wait_ge(dve_step, 1)
                dve.sem_inc(dve_step, -1)
                v.tensor_tensor(gsq[:, :], gm[:, :, 0], gm[:, :, 0], ALU.mult).then_inc(dve_step, 1)
                dve.wait_ge(dve_step, 1)
                dve.sem_inc(dve_step, -1)
                v.tensor_tensor(gvar[:, :], gm[:, :, 1], gsq[:, :], ALU.subtract).then_inc(dve_step, 1)
                dve.wait_ge(dve_step, 1)
                dve.sem_inc(dve_step, -1)
                v.tensor_scalar(grs[:, :], gvar[:, :], EPS, None, ALU.add).then_inc(dve_step, 1)
                dve.wait_ge(dve_step, 1)
                dve.sem_inc(dve_step, -1)
                dve.sem_inc(root_in, 1)
                dve.wait_ge(root_ready, 1)
                dve.sem_inc(root_ready, -1)
                v.tensor_tensor(gsc[:, :], grs[:, :], vec_s[:, gamma, :], ALU.mult).then_inc(dve_step, 1)
                dve.wait_ge(dve_step, 1)
                dve.sem_inc(dve_step, -1)
                v.tensor_tensor(gtm[:, :], gm[:, :, 0], gsc[:, :], ALU.mult).then_inc(dve_step, 1)
                dve.wait_ge(dve_step, 1)
                dve.sem_inc(dve_step, -1)
                v.tensor_tensor(gbi[:, :], vec_s[:, beta, :], gtm[:, :], ALU.subtract).then_inc(dve_step, 1)
                dve.wait_ge(dve_step, 1)
                dve.sem_inc(dve_step, -1)

            def table_stage(stage, ntok, pv):
                with dve.Fori(0, NCH // 2) as n2:
                    for p in range(2):
                        dve.wait_ge(tp_ready, 1)
                        dve.sem_inc(tp_ready, -1)
                        dve.wait_ge(ts_free[p], 16 * 8)
                        dve.sem_inc(ts_free[p], -16 * 8)
                        v.tensor_copy(stage[p].rearrange("p a b -> p (a b)"), pv).then_inc(dve_step, 1)
                        dve.wait_ge(dve_step, 1)
                        dve.sem_inc(dve_step, -1)
                        dve.sem_inc(tp_free, 1)
                        dve.sem_inc(ts_ready, 1)
                        dve.sem_inc(stage_free, 1)

            def offsets_in(off, base, no):
                with dve.Fori(0, NCH) as blk:
                    dve.wait_ge(off_ready, 1)
                    dve.sem_inc(off_ready, -1)
                    v.tensor_tensor(off.rearrange("p a b -> p (a b)")[:, bass.ds(blk * 4 * no, 4 * no)],
                                        ps[:, 2, 0:4 * no],
                                        base.rearrange("p a b -> p (a b)")[:, bass.ds(blk * 4 * no, 4 * no)],
                                        ALU.add).then_inc(off_free, 1)

            def corners(off, co, fr, w4, idx, mask=None):
                v.tensor_scalar(co, off[:, :, 0:O3], 0.0, float(H + 1), ALU.max, ALU.min).then_inc(dve_step, 1)
                dve.wait_ge(dve_step, 1)
                dve.sem_inc(dve_step, -1)
                fl = w4.rearrange("p a k c -> p a (k c)")[:, :, 0:O3]
                whole = fr.bitcast(I32)
                v.tensor_copy(whole, co).then_inc(dve_step, 1)
                dve.wait_ge(dve_step, 1)
                dve.sem_inc(dve_step, -1)
                v.tensor_copy(fl, whole).then_inc(dve_step, 1)
                dve.wait_ge(dve_step, 1)
                dve.sem_inc(dve_step, -1)
                v.tensor_tensor(fr, fl, co, ALU.is_gt).then_inc(dve_step, 1)
                dve.wait_ge(dve_step, 1)
                dve.sem_inc(dve_step, -1)
                v.tensor_tensor(fl, fl, fr, ALU.subtract).then_inc(dve_step, 1)
                dve.wait_ge(dve_step, 1)
                dve.sem_inc(dve_step, -1)
                v.tensor_tensor(fr, co, fl, ALU.subtract).then_inc(dve_step, 1)
                dve.wait_ge(dve_step, 1)
                dve.sem_inc(dve_step, -1)
                fl2 = fl.rearrange("p a (k two) -> p a k two", two=2)
                cy = co.rearrange("p a (k two) -> p a k two", two=2)
                fy = fr.rearrange("p a (k two) -> p a k two", two=2)
                v.scalar_tensor_tensor(co[:, :, 0:KK], fl2[:, :, :, 0], float(TY), fl2[:, :, :, 1],
                                            op0=ALU.mult, op1=ALU.add).then_inc(dve_step, 1)
                dve.wait_ge(dve_step, 1)
                dve.sem_inc(dve_step, -1)
                v.tensor_copy(idx, co[:, :, 0:KK]).then_inc(dve_step, 1)
                dve.wait_ge(dve_step, 1)
                dve.sem_inc(dve_step, -1)
                v.tensor_scalar(co, fr, -1.0, 1.0, ALU.mult, ALU.add).then_inc(dve_step, 1)
                dve.wait_ge(dve_step, 1)
                dve.sem_inc(dve_step, -1)
                if mask is not None:
                    dve.wait_ge(mask_ready, 1)
                    dve.sem_inc(mask_ready, -1)
                    for part in (cy, fy):
                        v.tensor_tensor(part[:, :, :, 0], part[:, :, :, 0], mask, ALU.mult).then_inc(dve_step, 1)
                        dve.wait_ge(dve_step, 1)
                        dve.sem_inc(dve_step, -1)
                v.tensor_tensor(w4[:, :, :, 0], cy[:, :, :, 0], cy[:, :, :, 1], ALU.mult).then_inc(dve_step, 1)
                dve.wait_ge(dve_step, 1)
                dve.sem_inc(dve_step, -1)
                v.tensor_tensor(w4[:, :, :, 1], cy[:, :, :, 0], fy[:, :, :, 1], ALU.mult).then_inc(dve_step, 1)
                dve.wait_ge(dve_step, 1)
                dve.sem_inc(dve_step, -1)
                v.tensor_tensor(w4[:, :, :, 2], fy[:, :, :, 0], cy[:, :, :, 1], ALU.mult).then_inc(dve_step, 1)
                dve.wait_ge(dve_step, 1)
                dve.sem_inc(dve_step, -1)
                v.tensor_tensor(w4[:, :, :, 3], fy[:, :, :, 0], fy[:, :, :, 1], ALU.mult).then_inc(dve_step, 1)
                dve.wait_ge(dve_step, 1)
                dve.sem_inc(dve_step, -1)

            with dve.Fori(0, B) as b:
                dve.wait_ge(x_loaded, 16)
                dve.sem_inc(x_loaded, -16)
                group_norm(X[:, :, :], GN0_G, GN0_B)
                dve.sem_inc(scalar_in, 1)
                v.tensor_scalar(X[:, 0, :], X[:, 0, :], gsc[:, 0:1], gbi[:, 0:1], ALU.mult, ALU.add).then_inc(dve_step, 1)
                dve.wait_ge(dve_step, 1)
                dve.sem_inc(dve_step, -1)
                dve.drain().then_inc(arrived, 1)
                dve.wait_ge(go_dve, 1)
                dve.sem_inc(go_dve, -1)
                for j in range(NT // 2):
                    dve.wait_ge(v1_done, 1)
                    dve.sem_inc(v1_done, -1)
                    at = slice(2 * j * NHEAD, 2 * (j + 1) * NHEAD)
                    v.scalar_tensor_tensor(V[:, at, 1, :], ps[:, j % 4, :].rearrange("p (a d) -> p a d", d=D),
                                               V_SCALE, V[:, at, 0, :], op0=ALU.mult, op1=ALU.subtract).then_inc(v_free, 1)
                dve.drain().then_inc(arrived, 1)
                dve.wait_ge(go_dve, 1)
                dve.sem_inc(go_dve, -1)
                with dve.Fori(0, NHEAD) as h:
                    with dve.Fori(0, NCH // 2) as n2:
                        for p in range(2):
                            at = chunk(2 * n2 + p)
                            dve.wait_ge(qa_done, 1)
                            dve.sem_inc(qa_done, -1)
                            v.scalar_tensor_tensor(QB[:, at], ps[:, 2 * p, :], QK_SCALE, QA[:, at],
                                                       op0=ALU.mult, op1=ALU.subtract).then_inc(q_free, 1)
                            dve.wait_ge(ka_done, 1)
                            dve.sem_inc(ka_done, -1)
                            v.scalar_tensor_tensor(KA[64:128, at], ps[64:128, 2 * p + 1, :], QK_SCALE,
                                                       KA[64:128, at], op0=ALU.mult, op1=ALU.subtract).then_inc(k_free, 1)
                    dve.drain().then_inc(arrived, 1)
                    dve.wait_ge(go_dve, 1)
                    dve.sem_inc(go_dve, -1)

                    def score_in(p, g):
                        dve.wait_ge(score_ready, 1)
                        dve.sem_inc(score_ready, -1)
                        v.tensor_scalar(S[p][:, g * CHUNK:(g + 1) * CHUNK], ps[:, g % 2, :],
                                            float(D) ** -0.5 / QK_SCALE ** 2, -3.0e38, ALU.mult, ALU.max,
                                            accum_out=mx[p][:, g:g + 1]).then_inc(score_free if g < 7 else row_done, 1)

                    def maximum(p):
                        dve.wait_ge(row_done, 1)
                        dve.sem_inc(row_done, -1)
                        dve.sem_inc(score_free, 1)
                        v.tensor_reduce(nmx[p], mx[p], AX.X, ALU.max, negate=True).then_inc(dve_step, 1)
                        dve.wait_ge(dve_step, 1)
                        dve.sem_inc(dve_step, -1)
                        v.tensor_scalar(nmx[p], nmx[p], LN_P_MAX, None, ALU.add).then_inc(max_ready, 1)

                    def slot(p, ahead=True):
                        for g in range(8):
                            if ahead:
                                score_in(p, g)
                            dve.wait_ge(p1_ready, 1)
                            dve.sem_inc(p1_ready, -1)
                            v.tensor_tensor(P2[:, g % 4, :], ps[:, 2 + g % 4, :], P1[:, g % 4, :], ALU.subtract).then_inc(p2_ready, 1)
                        v.tensor_reduce(rsum[p], rs[p], AX.X, ALU.add).then_inc(dve_step, 1)
                        dve.wait_ge(dve_step, 1)
                        dve.sem_inc(dve_step, -1)
                        v.reciprocal(rr[p], rsum[p]).then_inc(rr_ready, 1)
                        if ahead:
                            maximum(p)

                    for p in range(2):
                        for g in range(8):
                            score_in(p, g)
                        maximum(p)
                    with dve.Fori(0, NT // 2 - 1) as t2:
                        slot(0)
                        slot(1)
                    slot(0, ahead=False)
                    slot(1, ahead=False)
                    dve.drain().then_inc(arrived, 1)
                    dve.wait_ge(go_dve, 1)
                    dve.sem_inc(go_dve, -1)
                with dve.Fori(0, NCH // 2) as n2:
                    for p in range(2):
                        dve.wait_ge(at_ps0, 1)
                        dve.sem_inc(at_ps0, -1)
                        v.tensor_copy(AT[:, 0, :], ps[:, 0, :]).then_inc(at_ready0, 1)
                        for oh in range(CH):
                            at = chunk(2 * n2 + p)
                            dve.wait_ge(proj_ready, 1)
                            dve.sem_inc(proj_ready, -1)
                            if oh == CH - 1:
                                dve.sem_inc(aol_free, 1)
                            v.tensor_tensor(X[:, oh, at], ps[:, 2 + oh, :], X[:, oh, at], ALU.add).then_inc(proj_free, 1)
                dve.drain().then_inc(arrived, 1)
                dve.wait_ge(go_dve, 1)
                dve.sem_inc(go_dve, -1)
                dve.wait_ge(x_loaded, 16)
                dve.sem_inc(x_loaded, -16)
                v.tensor_tensor(BASE2, BASE2, boff_s[:, :].unsqueeze(1).to_broadcast([128, NT, O2]), ALU.add).then_inc(dve_step, 1)
                dve.wait_ge(dve_step, 1)
                dve.sem_inc(dve_step, -1)
                dve.drain().then_inc(arrived, 1)
                dve.wait_ge(go_dve, 1)
                dve.sem_inc(go_dve, -1)
                table_stage(TS2, 1, ps[:, 2, 0:4 * CB])
                dve.drain().then_inc(arrived, 1)
                dve.wait_ge(go_dve, 1)
                dve.sem_inc(go_dve, -1)
                offsets_in(OFF2, BASE2, O2)
                dve.drain().then_inc(arrived, 1)
                dve.wait_ge(go_dve, 1)
                dve.sem_inc(go_dve, -1)
                corners(OFF2, CO2, FR2, W4_2, IDX2, MASK2)
                dve.drain().then_inc(arrived, 1)
                dve.wait_ge(go_dve, 1)
                dve.sem_inc(go_dve, -1)
                with dve.Fori(0, NT // 2) as t2:
                    for p in range(2):
                        t = 2 * t2 + p
                        v.tensor_copy(WS2[p], W4_2.rearrange("p a k c -> p (a k c)")[:, bass.ds(t * KK * 4, KK * 4)]).then_inc(dve_step, 1)
                        dve.wait_ge(dve_step, 1)
                        dve.sem_inc(dve_step, -1)
                        dve.wait_ge(g2_ready[p], (b * (NT // 2) + t2 + 1) * 16 * KK)
                        dve.sem_inc(gathers_seen, 1)
                        corner4 = G2[p].rearrange("p k (q c) -> p (k q) c", q=4)
                        v.tensor_tensor(corner4, corner4,
                                             WS2[p].unsqueeze(2).to_broadcast([128, KK * 4, CB]), ALU.mult).then_inc(dve_step, 1)
                        dve.wait_ge(dve_step, 1)
                        dve.sem_inc(dve_step, -1)
                        v.tensor_tensor(A2, G2[p][:, :, 0:2 * CB], G2[p][:, :, 2 * CB:4 * CB], ALU.add).then_inc(dve_step, 1)
                        dve.wait_ge(dve_step, 1)
                        dve.sem_inc(dve_step, -1)
                        dve.sem_inc(g2_free, 1)
                        dve.wait_ge(sm_free, 1)
                        dve.sem_inc(sm_free, -1)
                        v.tensor_tensor(SM2[p][:, 0:KK * CB].rearrange("p (k c) -> p k c", k=KK),
                                            A2[:, :, 0:CB], A2[:, :, CB:2 * CB], ALU.add).then_inc(sm_ready, 1)
                        dve.wait_ge(e_ready, 1)
                        dve.sem_inc(e_ready, -1)
                        at = bass.ds(t * 128, 128)
                        for oh in range(CH):
                            last = v.scalar_tensor_tensor(X[:, oh, at], ps[:, 3 + p, oh * 128:(oh + 1) * 128],
                                                          bn3s[:, oh:oh + 1], X[:, oh, at],
                                                          op0=ALU.mult, op1=ALU.add)
                        last.then_inc(dve_step, 1)
                        dve.wait_ge(dve_step, 1)
                        dve.sem_inc(dve_step, -1)
                        dve.sem_inc(e_free, 1)
                dve.drain().then_inc(arrived, 1)
                dve.wait_ge(go_dve, 1)
                dve.sem_inc(go_dve, -1)
                v.tensor_scalar(X[:, 1, :], X[:, 1, :], bn3b[:, 1:2], 0.0, ALU.add, ALU.max).then_inc(dve_step, 1)
                dve.wait_ge(dve_step, 1)
                dve.sem_inc(dve_step, -1)
                dve.drain().then_inc(arrived, 1)
                dve.wait_ge(go_dve, 1)
                dve.sem_inc(go_dve, -1)
                for layer in range(2):
                    group_norm(X[:, :, :] if layer == 0 else OUT, (GN1_G, GN2_G)[layer], (GN1_B, GN2_B)[layer])
                    for half in range(CH):
                        v.tensor_tensor(WO[:, half, :, :].rearrange("p a (b o) -> p (a b) o", o=O3),
                                             dw_s[:, layer, half, :].unsqueeze(2).to_broadcast([128, 49, O3]),
                                             pw_s[:, layer, half, :].unsqueeze(1).to_broadcast([128, 49, O3]),
                                             ALU.mult).then_inc(dve_step, 1)
                        dve.wait_ge(dve_step, 1)
                        dve.sem_inc(dve_step, -1)
                    dve.drain().then_inc(arrived, 1)
                    dve.wait_ge(go_dve, 1)
                    dve.sem_inc(go_dve, -1)
                    table_stage(TS3, 2, psf[:, 0:4 * C])
                    dve.drain().then_inc(arrived, 1)
                    dve.wait_ge(go_dve, 1)
                    dve.sem_inc(go_dve, -1)
                    dve.wait_ge(wd_loaded, 32)
                    v.tensor_tensor(BASE3, BASE3, pwb_s[:, layer, :].unsqueeze(1).to_broadcast([128, NT, O3]),
                                         ALU.add).then_inc(dve_step, 1)
                    dve.wait_ge(dve_step, 1)
                    dve.sem_inc(dve_step, -1)
                    offsets_in(OFF3, BASE3, O3)
                    dve.drain().then_inc(arrived, 1)
                    dve.wait_ge(go_dve, 1)
                    dve.sem_inc(go_dve, -1)
                    corners(OFF3, OFF3, FR3, W4_3, IDX3)
                    dve.drain().then_inc(arrived, 1)
                    dve.wait_ge(go_dve, 1)
                    dve.sem_inc(go_dve, -1)
                    with dve.Fori(0, NCH // 2) as g2:
                        for p in range(2):
                            g = 2 * g2 + p
                            v.tensor_copy(WS3[p], W4_3.rearrange("p a k c -> p (a k c)")
                                               [:, bass.ds(g * 4 * KK * 4, 4 * KK * 4)]).then_inc(dve_step, 1)
                            dve.wait_ge(dve_step, 1)
                            dve.sem_inc(dve_step, -1)
                            for k in range(KK):
                                par = (KK * p + k) % 2
                                dve.wait_ge(samp_free, 1)
                                dve.sem_inc(samp_free, -1)
                                uses = (g2 + (2 * b + layer) * (NCH // 2)) * KK + (KK * p + k) // 2 + 1
                                dve.wait_ge(g_ready[par], uses * 16 * 4)
                                dve.sem_inc(gathers_seen, 1)
                                for corner in range(4):
                                    for t in range(4):
                                        slot = 4 * par + t
                                        wcol = (t * KK + k) * 4 + corner
                                        weight = WS3[p][:, wcol:wcol + 1]
                                        sample = SAMP[par][:, t, :]
                                        if corner == 0:
                                            ins = v.tensor_scalar(sample, G3[slot][:, 0, :], weight, None, ALU.mult)
                                        else:
                                            dve.wait_ge(chain, 4 * (corner - 1) + t + 1)
                                            ins = v.scalar_tensor_tensor(sample, G3[slot][:, corner, :], weight, sample,
                                                                         op0=ALU.mult, op1=ALU.add)
                                        ins.then_inc(chain if corner < 3 else samp_ready, 1)
                                dve.sem_inc(chain, -12)
                            if layer == 1:
                                for oh in range(CH):
                                    dve.wait_ge(o_ready_dve, 1)
                                    dve.sem_inc(o_ready_dve, -1)
                                    at = chunk(g)
                                    v.scalar_tensor_tensor(OUT[:, oh, at], ps[:, 4 + 2 * p + oh, :],
                                                                vec_s[:, B2, oh:oh + 1], X[:, oh, at],
                                                                op0=ALU.add, op1=ALU.add).then_inc(dve_step, 1)
                                    dve.wait_ge(dve_step, 1)
                                    dve.sem_inc(dve_step, -1)
                                    dve.sem_inc(o_free, 1)
                                    dve.sem_inc(fo_ready, 1)
                                dve.sem_inc(st_free, 1)
                    dve.drain().then_inc(arrived, 1)
                    dve.wait_ge(go_dve, 1)
                    dve.sem_inc(go_dve, -1)


def constants():
    ident = np.eye(128, dtype=np.float32)
    mean32 = np.kron(np.eye(4), np.full((32, 32), 1 / 32)).astype(np.float32)
    mean8 = np.kron(np.eye(16), np.full((8, 8), 1 / 8)).astype(np.float32)
    sel2 = np.zeros((3 * O2, 3, O2), np.float32)
    sel3 = np.zeros((7 * O3, 7, O3), np.float32)
    for sel, ks, no in ((sel2, 3, O2), (sel3, 7, O3)):
        for kx in range(ks):
            for o in range(no):
                sel[kx * no + o, kx, o] = 1.0
    pix = np.arange(PIX).reshape(NT, 128).T
    grid = np.zeros((128, NT, KK, 2), np.float32)
    for k in range(KK):
        grid[:, :, k, 0] = pix // W - 1 + k // 3 + 1
        grid[:, :, k, 1] = pix % W - 1 + k % 3 + 1
    base3 = grid.reshape(128, NT, O3)
    base2 = np.concatenate([base3, np.zeros((128, NT, KK), np.float32)], axis=2)
    one = np.float32(1)
    jj = np.arange(W, dtype=np.float32) / np.float32(W - 1)
    ii = np.arange(H, dtype=np.float32) / np.float32(H - 1)
    at = np.arange(C)[None, :] * NPOS + np.arange(NPOS)[:, None]
    pos = np.stack([jj[at % W], ii[at // W], one - jj[at % W], one - ii[at // W], np.ones(at.shape, np.float32)])
    return ident, mean32, mean8, sel2, sel3, base2, base3, pos.astype(np.float32)


def kernel(**a):
    import concourse.bacc as bacc
    from concourse.bass_utils import run_bass_kernel_spmd

    a = {k: np.asarray(v) for k, v in a.items()}
    ident, mean32, mean8, sel2, sel3, base2, base3, pos = constants()
    halves = lambda m: np.ascontiguousarray(m.reshape(CH, 128, -1).transpose(1, 0, 2))
    vec = np.stack([a[n] for n in ("L0_conv_gn_gamma", "L0_conv_gn_beta", "L2_conv_bn3_g", "L2_conv_bn3_b",
                                   "L2_conv_bn3_m", "L2_conv_bn3_v", "L3_conv_gn1_g", "L3_conv_gn1_b", "L3_conv_b1",
                                   "L3_conv_gn2_g", "L3_conv_gn2_b", "L3_conv_b2")])
    vec64 = np.stack([a["L2_conv_" + n] for n in ("bn1_g", "bn1_b", "bn1_m", "bn1_v", "dcn_b", "bn2_g", "bn2_b",
                                                  "bn2_m", "bn2_v")], axis=1)
    arrays = {
        "x": a["x"].reshape(B, C, PIX),
        "wqkv": halves(a["L0_conv_w_qkv"].T),
        "wproj": halves(a["L0_conv_w_proj"].T),
        "pos_l": np.concatenate([pos, np.tile(a["L0_conv_b_proj"], (NPOS, 1))[None]], axis=0),
        "pos_r": np.concatenate([a["L1_conv_W"].T, a["L1_conv_b"][None], np.ones((1, C), np.float32)], axis=0),
        "vec": vec.reshape(12, CH, 128).transpose(2, 0, 1),
        "vec64": vec64,
        "w1": halves(a["L2_conv_w1"].T),
        "woff": a["L2_conv_woff"].transpose(1, 2, 3, 0).reshape(CB, 3, 3 * O2),
        "boff": np.tile(a["L2_conv_boff"], (128, 1)),
        "w2": a["L2_conv_w2"].transpose(2, 3, 1, 0).reshape(KK * CB, CB),
        "w3": a["L2_conv_w3"].T,
        "dw": np.stack([a[f"L3_conv_dw{i}"].reshape(CH, 128, 49) for i in (1, 2)]).transpose(2, 0, 1, 3),
        "pw": np.stack([a[f"L3_conv_pw{i}"].reshape(O3, CH, 128).transpose(1, 2, 0) for i in (1, 2)])
              .transpose(2, 0, 1, 3),
        "pwb": np.tile(np.stack([a["L3_conv_pwb1"], a["L3_conv_pwb2"]])[None], (128, 1, 1)),
        "wd": np.stack([a[f"L3_conv_w{i}"].reshape(C, CH, 128, KK).transpose(2, 3, 1, 0) for i in (1, 2)]),
        "ident": ident, "mean32": mean32, "mean8": mean8, "sel2": sel2, "sel3": sel3, "base2": base2,
        "base3": base3,
    }
    arrays = {"in_" + k: np.ascontiguousarray(v) for k, v in arrays.items()}
    nc = bacc.Bacc("TRN2", target_bir_lowering=False, num_devices=1)
    args = [nc.dram_tensor(k, v.shape, mybir.dt.from_np(v.dtype), kind="ExternalInput").ap()
            for k, v in arrays.items()]
    out = nc.dram_tensor("out_y", (B, C, PIX), F32, kind="ExternalOutput").ap()
    order = [k[3:] for k in arrays]
    named = dict(zip(order, args))
    program(nc, out=out, **named)
    got = run_bass_kernel_spmd(nc, [arrays], core_ids=[0])
    return got.results[0]["out_y"].reshape(B, C, H, W)
```

```python
from contextlib import ExitStack

import numpy as np

import concourse.bass as bass
from concourse import mybir

F32, F16, I32 = mybir.dt.float32, mybir.dt.float16, mybir.dt.int32
ALU = mybir.AluOpType
ACT = mybir.ActivationFunctionType
AX = mybir.AxisListType

B, C, H, W = 2, 256, 64, 64
PIX = H * W
CH = C // 128
NT = PIX // 128
NHEAD, D = 4, 64
CB = 64
EPS = 1e-5
CHUNK = 512
NCH = PIX // CHUNK
TY = H + 2
KK = 9
PW2, PW7 = W + 2, W + 6
O2, O3 = 27, 18
QK_SCALE, V_SCALE = 16.0, 64.0
LN_P_MAX = 14 * float(np.log(2.0))
NPOS = PIX // C

GN0_G, GN0_B, BN3_G, BN3_B, BN3_M, BN3_V, GN1_G, GN1_B, B1, GN2_G, GN2_B, B2 = range(12)
BN1_G, BN1_B, BN1_M, BN1_V, DCN_B, BN2_G, BN2_B, BN2_M, BN2_V = range(9)


def program(nc, x, wqkv, wproj, pos_l, pos_r, vec, vec64, w1, woff, boff, w2, w3, dw, pw, pwb, wd,
            ident, mean32, mean8, sel2, sel3, base2, base3, out):
    ctx = ExitStack()
    with ctx:
        def sb(name, shape, dt=F32):
            return ctx.enter_context(nc.sbuf_tensor(name, shape, dt))

        def sem(name):
            return ctx.enter_context(nc.semaphore(name))

        attn_dram = nc.dram_tensor("attn_scratch", (PIX, C), F32, kind="Internal").ap()
        table64 = nc.dram_tensor("corners64", (TY * TY, 4 * CB), F32, kind="Internal").ap()
        table256 = nc.dram_tensor("corners256", (TY * TY, 4 * C), F32, kind="Internal").ap()

        X = sb("X", [128, CH, PIX])
        wqkv_s = sb("wqkv_s", [128, CH, 3 * C])
        wproj_s = sb("wproj_s", [128, CH, C])
        pos_r_s = sb("pos_r_s", [6, C])
        vec_s = sb("vec_s", [128, 12, CH])
        vec64_s = sb("vec64_s", [CB, 9])
        w1_s = sb("w1_s", [128, CH, CB])
        woff_s = sb("woff_s", [CB, 3, 3 * O2])
        w2_s = sb("w2_s", [128, 5, CB])
        w3_s = sb("w3_s", [CB, C])
        dw_s = sb("dw_s", [128, 2, CH, 49])
        pw_s = sb("pw_s", [128, 2, CH, O3])
        ident_s = sb("ident_s", [128, 128])
        mean32_s = sb("mean32_s", [128, 128])
        mean8_s = sb("mean8_s", [128, 128])
        sel2_s = sb("sel2_s", [3 * O2, 3 + O2])
        sel3_s = sb("sel3_s", [7 * O3, 7 + O3])
        boff_s = sb("boff_s", [128, O2])
        pwb_s = sb("pwb_s", [128, 2, O3])
        bnst = sb("bnst", [128, CH, 8, 6])
        mv = sb("mv", [128, CH, 2])
        gm = sb("gm", [128, CH, 2])
        gsq = sb("gsq", [128, CH])
        gvar = sb("gvar", [128, CH])
        grs = sb("grs", [128, CH])
        gsc = sb("gsc", [128, CH])
        gtm = sb("gtm", [128, CH])
        gbi = sb("gbi", [128, CH])
        bn3s = sb("bn3s", [128, CH])
        bn3b = sb("bn3b", [128, CH])
        bnf = sb("bnf", [CB, 8])
        minus_half = sb("minus_half", [128, CH])

        ARENA = 40300
        arena = sb("arena", [128, ARENA])

        class Carver:
            def __init__(self, start=0):
                self.at = start

            def f32(self, *dims, parts=128, dt=F32):
                n = int(np.prod(dims))
                words = n if dt != F16 else n // 2
                view = arena[0:parts, self.at:self.at + words]
                self.at += words
                assert self.at <= ARENA, self.at
                if dt != F32:
                    view = view.bitcast(dt)
                if len(dims) > 1:
                    names = "abcd"[:len(dims)]
                    view = view.rearrange(f"p ({' '.join(names)}) -> p {' '.join(names)}",
                                          **dict(zip(names, dims)))
                return view

        att = Carver()
        QA, QB, KA = (att.f32(2, PIX, dt=F16) for _ in range(3))
        KT = [att.f32(CHUNK, dt=F16) for _ in range(2)]
        V = att.f32(NT * NHEAD, 2, D, dt=F16)
        S = [att.f32(PIX) for _ in range(2)]
        P1 = att.f32(4, CHUNK, dt=F16)
        P2 = att.f32(4, CHUNK, dt=F16)
        WQK = att.f32(2, CH, 2 * D)
        O1 = [att.f32(2, D) for _ in range(2)]
        AO = [att.f32(D) for _ in range(2)]
        mx = [att.f32(8) for _ in range(2)]
        nmx = [att.f32(1) for _ in range(2)]
        rs = [att.f32(4) for _ in range(2)]
        rsum = [att.f32(1) for _ in range(2)]
        rr = [att.f32(1) for _ in range(2)]
        prj = Carver()
        AOL = [prj.f32(4, C) for _ in range(2)]
        POSL = [prj.f32(2, C, parts=6) for _ in range(2)]
        AT = prj.f32(CH, CHUNK)

        bot = Carver()
        HP2 = bot.f32(PW2 * PW2, parts=CB)
        STG2 = [bot.f32(CHUNK, parts=CB) for _ in range(2)]
        TS2 = [bot.f32(4, CB) for _ in range(2)]
        T2 = [bot.f32(CHUNK, parts=3 * O2) for _ in range(2)]
        BASE2 = bot.f32(NT, O2)
        OFF2 = bot.f32(NT, O2)
        MASK2 = bot.f32(NT, KK)
        FR2 = bot.f32(NT, O3)
        FL2 = bot.f32(NT, O3)
        CO2 = bot.f32(NT, O3)
        W4_2 = bot.f32(NT, KK, 4)
        IDX2 = bot.f32(NT, KK, dt=I32)
        G2 = [bot.f32(KK, 4 * CB) for _ in range(2)]
        IS2 = [bot.f32(KK, dt=I32) for _ in range(2)]
        WS2 = [bot.f32(KK * 4) for _ in range(2)]
        A2 = bot.f32(KK, 2 * CB)
        SM2 = [bot.f32(5 * 128) for _ in range(2)]
        SMT2 = [bot.f32(5, 128) for _ in range(2)]
        H2 = [bot.f32(128, parts=CB) for _ in range(2)]

        dcn = Carver()
        OUT = dcn.f32(CH, PIX)
        hole = dcn.at
        HP7 = dcn.f32(CH, PW7 * PW7)
        after = dcn.at
        WD = dcn.f32(KK, CH, C)
        WO = dcn.f32(CH, 7, 7 * O3)
        BASE3 = dcn.f32(NT, O3)
        T3 = [dcn.f32(CHUNK, parts=7 * O3) for _ in range(2)]
        OFF3 = dcn.f32(NT, O3)
        FR3 = dcn.f32(NT, O3)
        W4_3 = dcn.f32(NT, KK, 4)
        IDX3 = dcn.f32(NT, KK, dt=I32)
        IS3 = [dcn.f32(4, KK, dt=I32) for _ in range(2)]
        WS3 = [dcn.f32(4 * KK * 4) for _ in range(2)]
        stg = Carver(dcn.at)
        STG3 = [stg.f32(CH, CHUNK) for _ in range(2)]
        TS3 = [stg.f32(4, C) for _ in range(2)]
        SAMP = [dcn.f32(4, C) for _ in range(2)]
        ST = [dcn.f32(CH, CHUNK) for _ in range(2)]
        NG = 12
        ring = Carver(hole)
        in_hole = (after - hole) // (4 * C)
        G3 = [(ring if i < in_hole else dcn).f32(4, C) for i in range(NG)]
        ZERO = Carver().f32(4 * C)

        ps = ctx.enter_context(nc.psum_tensor("ps", [128, 8, CHUNK], F32))
        psf = ps[:, :, :].rearrange("p a b -> p (a b)")

        loaded = sem("loaded")
        dve_step = sem("dve_step")
        act_step = sem("act_step")
        pool_step = sem("pool_step")
        zeroed = sem("zeroed")
        x_loaded = sem("x_loaded")
        gn_stat = sem("gn_stat")
        gn_mean = sem("gn_mean")
        v_ready = sem("v_ready")
        v1_done = sem("v1_done")
        v_free = sem("v_free")
        wqk_ready = sem("wqk_ready")
        q_ready = sem("q_ready")
        k_ready = sem("k_ready")
        q_free = sem("q_free")
        k_free = sem("k_free")
        qa_done = sem("qa_done")
        ka_done = sem("ka_done")
        dup_ready = sem("dup_ready")
        dup_done = sem("dup_done")
        kt_free0 = sem("kt_free0")
        kt_free1 = sem("kt_free1")
        score_ready = sem("score_ready")
        score_free = sem("score_free")
        row_done = sem("row_done")
        max_ready = sem("max_ready")
        prob_ready = sem("prob_ready")
        tr_ready = sem("tr_ready")
        p1_ready = sem("p1_ready")
        p2_ready = sem("p2_ready")
        rr_ready = sem("rr_ready")
        out_ready = sem("out_ready")
        out_free = sem("out_free")
        o1_ready = sem("o1_ready")
        out_done = sem("out_done")
        ao_free0 = sem("ao_free0")
        ao_free1 = sem("ao_free1")
        aol_ready0 = sem("aol_ready0")
        aol_ready1 = sem("aol_ready1")
        aol_free = sem("aol_free")
        at_ps0 = sem("at_ps0")
        at_ps1 = sem("at_ps1")
        at_ready0 = sem("at_ready0")
        at_ready1 = sem("at_ready1")
        proj_ready = sem("proj_ready")
        proj_free = sem("proj_free")
        h1_ready = sem("h1_ready")
        h1_free = sem("h1_free")
        stage_ready = sem("stage_ready")
        stage_free = sem("stage_free")
        tp_ready = sem("tp_ready")
        tp_free = sem("tp_free")
        ts_ready = sem("ts_ready")
        ts_free0 = sem("ts_free0")
        ts_free1 = sem("ts_free1")
        image_ready = sem("image_ready")
        t_ps = sem("t_ps")
        t_ready = sem("t_ready")
        off_ready = sem("off_ready")
        off_free = sem("off_free")
        mask_ready = sem("mask_ready")
        g2_ready0 = sem("g2_ready0")
        g2_ready1 = sem("g2_ready1")
        g2_free = sem("g2_free")
        sm_ready = sem("sm_ready")
        sm_free = sem("sm_free")
        smt_ps = sem("smt_ps")
        smt_ready = sem("smt_ready")
        d_ready = sem("d_ready")
        h2_ready = sem("h2_ready")
        e_ready = sem("e_ready")
        e_free = sem("e_free")
        g_free = sem("g_free")
        chain = sem("chain")
        samp_ready = sem("samp_ready")
        st_ps = sem("st_ps")
        st_ready = sem("st_ready")
        st_free = sem("st_free")
        prod_ready = sem("prod_ready")
        o_ready = sem("o_ready")
        o_free = sem("o_free")
        out_filled = sem("out_filled")
        fo_ready = sem("fo_ready")
        fo_sent = sem("fo_sent")
        wd_loaded = sem("wd_loaded")
        arrived = sem("arrived")
        go_act = sem("go_act")
        go_dve = sem("go_dve")
        go_pe = sem("go_pe")
        go_pool = sem("go_pool")
        scalar_in = sem("scalar_in")
        root_in = sem("root_in")
        root_ready = sem("root_ready")
        gathers_seen = sem("gathers_seen")
        g_ready = [sem(f"g_ready{i}") for i in range(3)]
        ao_free = [ao_free0, ao_free1]
        kt_free = [kt_free0, kt_free1]
        aol_ready = [aol_ready0, aol_ready1]
        ts_free = [ts_free0, ts_free1]
        g2_ready = [g2_ready0, g2_ready1]

        def chunk(n):
            return bass.ds(n * CHUNK, CHUNK)

        block = ctx.enter_context(nc.Block())

        @block.sync
        def _(sp):
            loads = [(wqkv_s, wqkv), (wproj_s, wproj), (pos_r_s, pos_r), (vec_s, vec), (vec64_s, vec64),
                     (w1_s, w1), (woff_s, woff), (w3_s, w3), (dw_s, dw), (pw_s, pw), (ident_s, ident),
                     (mean32_s, mean32), (mean8_s, mean8), (sel2_s, sel2), (sel3_s, sel3), (boff_s, boff),
                     (pwb_s, pwb)]
            for dst, src in loads:
                sp.dma_start(dst[:], src).then_inc(loaded, 16)
            sp.wait_ge(zeroed, 1)
            sp.sem_inc(zeroed, -1)
            sp.dma_start(w2_s[:, 0:4, :], w2[0:512, :].rearrange("(a p) o -> p a o", p=128)).then_inc(loaded, 16)
            sp.dma_start(w2_s[0:CB, 4, :], w2[512:576, :]).then_inc(loaded, 16)
            n_loads = len(loads) + 2
            for tab, cc in ((table64, CB), (table256, C)):
                rows = tab.rearrange("(y x) c -> y x c", y=TY)
                for yy in (0, H, H + 1):
                    sp.dma_start(tab.rearrange("(y x) c -> y (x c)", y=TY)[yy, :].rearrange("(p f) -> p f", p=128),
                                     ZERO[:, 0:TY * 4 * cc // 128]).then_inc(loaded, 16)
                for xx in (0, W, W + 1):
                    sp.dma_start(rows[1:H, xx, :], ZERO[0:H - 1, 0:4 * cc]).then_inc(loaded, 16)
                n_loads += 6
            sp.wait_ge(loaded, 16 * n_loads)
            sp.sem_inc(loaded, -16 * n_loads)
            sp.drain().then_inc(arrived, 1)
            sp.wait_ge(arrived, 5)
            sp.sem_inc(arrived, -5)
            sp.sem_inc(go_act, 1)
            sp.sem_inc(go_dve, 1)
            sp.sem_inc(go_pe, 1)
            sp.sem_inc(go_pool, 1)

            def table_writes(p, n, stage, table, cc):
                sp.wait_ge(ts_ready, 1)
                sp.sem_inc(ts_ready, -1)
                rows = table.rearrange("(y x) (k c) -> y x k c", y=TY, k=4)
                for dy in range(2):
                    for dx in range(2):
                        for r in range(2):
                            dst = rows[bass.ds(8 * n + r + 1 - dy, 4, 2), 1 - dx:1 - dx + W, 2 * dy + dx, :]
                            sp.dma_start(dst.rearrange("y x c -> x y c"),
                                             stage[r * W:(r + 1) * W, :, :]).then_inc(ts_free[p], 16)

            with sp.Fori(0, B) as b:
                sp.dma_start(X[:, :, :], x[bass.ds(b, 1)].rearrange("o (a p) n -> p (o a) n", p=128)).then_inc(x_loaded, 16)
                sp.drain().then_inc(arrived, 1)
                sp.wait_ge(arrived, 5)
                sp.sem_inc(arrived, -5)
                sp.sem_inc(go_act, 1)
                sp.sem_inc(go_dve, 1)
                sp.sem_inc(go_pe, 1)
                sp.sem_inc(go_pool, 1)
                sp.drain().then_inc(arrived, 1)
                sp.wait_ge(arrived, 5)
                sp.sem_inc(arrived, -5)
                sp.sem_inc(go_act, 1)
                sp.sem_inc(go_dve, 1)
                sp.sem_inc(go_pe, 1)
                sp.sem_inc(go_pool, 1)
                with sp.Fori(0, NHEAD // 2) as pair:
                    with sp.Fori(0, NCH // 2) as n2:
                        for p in range(2):
                            at = chunk(2 * n2 + p)
                            sp.wait_ge(dup_ready, 1)
                            sp.sem_inc(dup_ready, -1)
                            for part in (QA, QB):
                                sp.dma_start(part[64:128, 0, at], part[0:64, 0, at]).then_inc(dup_done, 16)
                                sp.dma_start(part[0:64, 1, at], part[64:128, 1, at]).then_inc(dup_done, 16)
                            sp.dma_start(KA[64:128, 0, at], KT[p][0:64]).then_inc(kt_free[p], 16)
                            sp.dma_start(KA[0:64, 1, at], KT[p][64:128]).then_inc(kt_free[p], 16)
                    sp.wait_ge(dup_done, 64 * NCH)
                    sp.sem_inc(dup_done, -64 * NCH)
                    for p in range(2):
                        sp.wait_ge(kt_free[p], 32)
                    sp.drain().then_inc(arrived, 1)
                    sp.wait_ge(arrived, 5)
                    sp.sem_inc(arrived, -5)
                    sp.sem_inc(go_act, 1)
                    sp.sem_inc(go_dve, 1)
                    sp.sem_inc(go_pe, 1)
                    sp.sem_inc(go_pool, 1)
                    with sp.Fori(0, 2) as h2:
                        with sp.Fori(0, NT // 2) as t2:
                            for p in range(2):
                                sp.wait_ge(out_done, 1)
                                sp.sem_inc(out_done, -1)
                                sp.dma_start(attn_dram[bass.ds((2 * t2 + p) * 128, 128),
                                                           bass.ds((2 * pair + h2) * D, D)], AO[p]).then_inc(ao_free[p], 16)
                    for p in range(2):
                        sp.wait_ge(ao_free[p], 16)
                    sp.drain().then_inc(arrived, 1)
                    sp.wait_ge(arrived, 5)
                    sp.sem_inc(arrived, -5)
                    sp.sem_inc(go_act, 1)
                    sp.sem_inc(go_dve, 1)
                    sp.sem_inc(go_pe, 1)
                    sp.sem_inc(go_pool, 1)
                with sp.Fori(0, NCH // 2) as n2:
                    for p in range(2):
                        n = 2 * n2 + p
                        sp.wait_ge(aol_free, 1)
                        sp.sem_inc(aol_free, -1)
                        sp.dma_start(AOL[p], attn_dram[chunk(n), :].rearrange("(a p) c -> p a c", p=128)).then_inc(aol_ready[p], 16)
                        sp.dma_start(POSL[p], pos_l[:, bass.ds(2 * n, 2), :]).then_inc(aol_ready[p], 16)
                sp.drain().then_inc(arrived, 1)
                sp.wait_ge(arrived, 5)
                sp.sem_inc(arrived, -5)
                sp.sem_inc(go_act, 1)
                sp.sem_inc(go_dve, 1)
                sp.sem_inc(go_pe, 1)
                sp.sem_inc(go_pool, 1)
                sp.dma_start(BASE2, base2).then_inc(x_loaded, 16)
                sp.drain().then_inc(arrived, 1)
                sp.wait_ge(arrived, 5)
                sp.sem_inc(arrived, -5)
                sp.sem_inc(go_act, 1)
                sp.sem_inc(go_dve, 1)
                sp.sem_inc(go_pe, 1)
                sp.sem_inc(go_pool, 1)
                with sp.Fori(0, NCH // 2) as n2:
                    for p in range(2):
                        table_writes(p, 2 * n2 + p, TS2[p], table64, CB)
                for p in range(2):
                    sp.wait_ge(ts_free[p], 16 * 8)
                sp.drain().then_inc(arrived, 1)
                sp.wait_ge(arrived, 5)
                sp.sem_inc(arrived, -5)
                sp.sem_inc(go_act, 1)
                sp.sem_inc(go_dve, 1)
                sp.sem_inc(go_pe, 1)
                sp.sem_inc(go_pool, 1)
                sp.drain().then_inc(arrived, 1)
                sp.wait_ge(arrived, 5)
                sp.sem_inc(arrived, -5)
                sp.sem_inc(go_act, 1)
                sp.sem_inc(go_dve, 1)
                sp.sem_inc(go_pe, 1)
                sp.sem_inc(go_pool, 1)
                sp.drain().then_inc(arrived, 1)
                sp.wait_ge(arrived, 5)
                sp.sem_inc(arrived, -5)
                sp.sem_inc(go_act, 1)
                sp.sem_inc(go_dve, 1)
                sp.sem_inc(go_pe, 1)
                sp.sem_inc(go_pool, 1)
                sp.drain().then_inc(arrived, 1)
                sp.wait_ge(arrived, 5)
                sp.sem_inc(arrived, -5)
                sp.sem_inc(go_act, 1)
                sp.sem_inc(go_dve, 1)
                sp.sem_inc(go_pe, 1)
                sp.sem_inc(go_pool, 1)
                for layer in range(2):
                    sp.dma_start(WD, wd[layer]).then_inc(wd_loaded, 16)
                    sp.dma_start(BASE3, base3).then_inc(wd_loaded, 16)
                    sp.drain().then_inc(arrived, 1)
                    sp.wait_ge(arrived, 5)
                    sp.sem_inc(arrived, -5)
                    sp.sem_inc(go_act, 1)
                    sp.sem_inc(go_dve, 1)
                    sp.sem_inc(go_pe, 1)
                    sp.sem_inc(go_pool, 1)
                    with sp.Fori(0, NCH // 2) as n2:
                        for p in range(2):
                            table_writes(p, 2 * n2 + p, TS3[p], table256, C)
                    for p in range(2):
                        sp.wait_ge(ts_free[p], 16 * 8)
                    sp.drain().then_inc(arrived, 1)
                    sp.wait_ge(arrived, 5)
                    sp.sem_inc(arrived, -5)
                    sp.sem_inc(go_act, 1)
                    sp.sem_inc(go_dve, 1)
                    sp.sem_inc(go_pe, 1)
                    sp.sem_inc(go_pool, 1)
                    sp.wait_ge(wd_loaded, 32)
                    sp.sem_inc(wd_loaded, -32)
                    sp.drain().then_inc(arrived, 1)
                    sp.wait_ge(arrived, 5)
                    sp.sem_inc(arrived, -5)
                    sp.sem_inc(go_act, 1)
                    sp.sem_inc(go_dve, 1)
                    sp.sem_inc(go_pe, 1)
                    sp.sem_inc(go_pool, 1)
                    if layer == 1:
                        with sp.Fori(0, NCH) as g:
                            for oh in range(CH):
                                sp.wait_ge(fo_ready, 1)
                                sp.sem_inc(fo_ready, -1)
                                sp.dma_start(out[bass.ds(b, 1), oh * 128:(oh + 1) * 128, chunk(g)]
                                                 .rearrange("o p n -> p (o n)"), OUT[:, oh, chunk(g)]).then_inc(fo_sent, 16)
                        sp.wait_ge(fo_sent, 16 * NCH * CH)
                        sp.sem_inc(fo_sent, -16 * NCH * CH)
                    sp.drain().then_inc(arrived, 1)
                    sp.wait_ge(arrived, 5)
                    sp.sem_inc(arrived, -5)
                    sp.sem_inc(go_act, 1)
                    sp.sem_inc(go_dve, 1)
                    sp.sem_inc(go_pe, 1)
                    sp.sem_inc(go_pool, 1)

        @block.gpsimd
        def _(pool):
            pool.memset(w2_s[:, 4, :], 0.0).then_inc(pool_step, 1)
            pool.wait_ge(pool_step, 1)
            pool.sem_inc(pool_step, -1)
            pool.memset(minus_half[:, :], -0.5).then_inc(pool_step, 1)
            pool.wait_ge(pool_step, 1)
            pool.sem_inc(pool_step, -1)
            pool.memset(ZERO, 0.0).then_inc(pool_step, 1)
            pool.wait_ge(pool_step, 1)
            pool.sem_inc(pool_step, -1)
            pool.sem_inc(zeroed, 1)
            pool.drain().then_inc(arrived, 1)
            pool.wait_ge(go_pool, 1)
            pool.sem_inc(go_pool, -1)

            def inverse_root(ap):
                pool.wait_ge(root_in, 1)
                pool.sem_inc(root_in, -1)
                pool.tensor_tensor(ap, ap, minus_half[0:ap.shape[0], 0:ap.shape[1]], ALU.pow).then_inc(root_ready, 1)

            inverse_root(bnf[:, 0:1])
            inverse_root(bnf[:, 2:3])
            inverse_root(bn3s[:, :])
            with pool.Fori(0, B) as b:
                inverse_root(grs[:, :])
                pool.drain().then_inc(arrived, 1)
                pool.wait_ge(go_pool, 1)
                pool.sem_inc(go_pool, -1)
                pool.drain().then_inc(arrived, 1)
                pool.wait_ge(go_pool, 1)
                pool.sem_inc(go_pool, -1)
                with pool.Fori(0, NHEAD // 2) as pair:
                    for qk in range(2):
                        pool.tensor_copy(WQK[:, qk, :, :], wqkv_s[:, :, bass.ds(qk * C + pair * 2 * D, 2 * D)]).then_inc(wqk_ready, 1)
                    pool.drain().then_inc(arrived, 1)
                    pool.wait_ge(go_pool, 1)
                    pool.sem_inc(go_pool, -1)
                    with pool.Fori(0, NT) as t2:
                        for p in range(2):
                            pool.wait_ge(o1_ready, 1)
                            pool.sem_inc(o1_ready, -1)
                            pool.wait_ge(ao_free[p], 16)
                            pool.sem_inc(ao_free[p], -16)
                            pool.tensor_tensor(AO[p], O1[p][:, 0, :], O1[p][:, 1, :], ALU.add).then_inc(pool_step, 1)
                            pool.wait_ge(pool_step, 1)
                            pool.sem_inc(pool_step, -1)
                            pool.sem_inc(out_free, 1)
                            pool.tensor_scalar(AO[p], AO[p], 1.0 / V_SCALE, None, ALU.mult).then_inc(out_done, 1)
                    pool.drain().then_inc(arrived, 1)
                    pool.wait_ge(go_pool, 1)
                    pool.sem_inc(go_pool, -1)
                pool.drain().then_inc(arrived, 1)
                pool.wait_ge(go_pool, 1)
                pool.sem_inc(go_pool, -1)
                pool.memset(HP2, 0.0).then_inc(pool_step, 1)
                pool.wait_ge(pool_step, 1)
                pool.sem_inc(pool_step, -1)
                for p in range(2):
                    pool.memset(SM2[p], 0.0).then_inc(pool_step, 1)
                    pool.wait_ge(pool_step, 1)
                    pool.sem_inc(pool_step, -1)
                pool.drain().then_inc(arrived, 1)
                pool.wait_ge(go_pool, 1)
                pool.sem_inc(go_pool, -1)
                pool.drain().then_inc(arrived, 1)
                pool.wait_ge(go_pool, 1)
                pool.sem_inc(go_pool, -1)
                pool.drain().then_inc(arrived, 1)
                pool.wait_ge(go_pool, 1)
                pool.sem_inc(go_pool, -1)
                with pool.Fori(0, NT // 2) as t2:
                    for p in range(2):
                        pool.wait_ge(g2_free, 1)
                        pool.sem_inc(g2_free, -1)
                        pool.tensor_copy(IS2[p], IDX2[:, bass.ds(2 * t2 + p, 1), :]
                                                                 .rearrange("p a k -> p (a k)")).then_inc(pool_step, 1)
                        pool.wait_ge(pool_step, 1)
                        pool.sem_inc(pool_step, -1)
                        for k in range(KK):
                            pool.indirect_dma_start(G2[p][:, k, :], None, table64,
                                                        bass.IndirectOffsetOnAxis(ap=IS2[p][:, k:k + 1], axis=0)).then_inc(g2_ready[p], 16)
                pool.drain().then_inc(arrived, 1)
                pool.wait_ge(go_pool, 1)
                pool.sem_inc(go_pool, -1)
                pool.drain().then_inc(arrived, 1)
                pool.wait_ge(go_pool, 1)
                pool.sem_inc(go_pool, -1)
                for layer in range(2):
                    pool.memset(HP7.rearrange("p a n -> p (a n)"), 0.0).then_inc(pool_step, 1)
                    pool.wait_ge(pool_step, 1)
                    pool.sem_inc(pool_step, -1)
                    inverse_root(grs[:, :])
                    pool.drain().then_inc(arrived, 1)
                    pool.wait_ge(go_pool, 1)
                    pool.sem_inc(go_pool, -1)
                    pool.drain().then_inc(arrived, 1)
                    pool.wait_ge(go_pool, 1)
                    pool.sem_inc(go_pool, -1)
                    pool.drain().then_inc(arrived, 1)
                    pool.wait_ge(go_pool, 1)
                    pool.sem_inc(go_pool, -1)
                    with pool.Fori(0, NCH // 2) as g2:
                        for p in range(2):
                            pool.tensor_copy(
                                IS3[p].rearrange("p a k -> p (a k)"),
                                IDX3.rearrange("p a k -> p (a k)")[:, bass.ds((2 * g2 + p) * 4 * KK, 4 * KK)]).then_inc(pool_step, 1)
                            pool.wait_ge(pool_step, 1)
                            pool.sem_inc(pool_step, -1)
                            pool.tensor_copy(
                                WS3[p], W4_3.rearrange("p a k c -> p (a k c)")
                                [:, bass.ds((2 * g2 + p) * 4 * KK * 4, 4 * KK * 4)]).then_inc(pool_step, 1)
                            pool.wait_ge(pool_step, 1)
                            pool.sem_inc(pool_step, -1)
                            for k in range(KK):
                                for t in range(4):
                                    slot = 4 * (k % 3) + t
                                    pool.wait_ge(g_free, 1)
                                    pool.sem_inc(g_free, -1)
                                    pool.indirect_dma_start(
                                        G3[slot].rearrange("p a c -> p (a c)"), None, table256,
                                        bass.IndirectOffsetOnAxis(ap=IS3[p][:, t, k:k + 1], axis=0)).then_inc(g_ready[k % 3], 16)
                    pool.drain().then_inc(arrived, 1)
                    pool.wait_ge(go_pool, 1)
                    pool.sem_inc(go_pool, -1)

        @block.tensor
        def _(pe):
            mm, tr = nc.tensor.matmul, nc.tensor.transpose
            pe.drain().then_inc(arrived, 1)
            pe.wait_ge(go_pe, 1)
            pe.sem_inc(go_pe, -1)

            def gn_means(groups):
                pe.wait_ge(gn_stat, 1)
                pe.sem_inc(gn_stat, -1)
                mm(ps[:, 7, 0:2 * CH], groups[:, :], mv[:, :, :].rearrange("p a b -> p (a b)"),
                       start=True, stop=True).then_inc(gn_mean, 1)

            def offset_conv(table, img, halves, pw_, ksize, wts, tbuf, no, sel):
                ko = ksize * no
                n = 4 * pw_

                def rows(blk, p):
                    pe.wait_ge(image_ready, 1)
                    pe.sem_inc(image_ready, -1)
                    for j in range(2):
                        first = True
                        for half in range(halves):
                            for ky in range(ksize):
                                last = mm(ps[0:ko, 2 + 2 * p + j, 0:n], wts(half, ky),
                                          img(half)[:, bass.ds((8 * blk + 4 * j + ky) * pw_, n)],
                                          start=first, stop=(half == halves - 1 and ky == ksize - 1))
                                first = False
                        last.then_inc(t_ps, 1)

                def shifted(p):
                    pe.wait_ge(t_ready, 2)
                    pe.sem_inc(t_ready, -2)
                    pe.wait_ge(off_free, 1)
                    pe.sem_inc(off_free, -1)
                    for t in range(4):
                        last = mm(ps[:, 6 + p, t * no:(t + 1) * no], tbuf[p][:, t * 128:(t + 1) * 128],
                                  sel[:, ksize:ksize + no], start=True, stop=True)
                    last.then_inc(off_ready, 1)

                table(0, 0)
                table(1, 1)
                rows(0, 0)
                with pe.Fori(0, NCH // 2 - 2) as n2:
                    for p in range(2):
                        table(2 * n2 + 2 + p, p)
                        rows(2 * n2 + 1 + p, 1 - p)
                        shifted(p)
                for p in range(2):
                    table(NCH - 2 + p, p)
                    rows(NCH - 3 + p, 1 - p)
                    shifted(p)
                rows(NCH - 1, 1)
                shifted(0)
                shifted(1)

            with pe.Fori(0, B) as b:
                gn_means(mean32_s)
                pe.drain().then_inc(arrived, 1)
                pe.wait_ge(go_pe, 1)
                pe.sem_inc(go_pe, -1)
                for j in range(NT // 2):
                    pe.wait_ge(v_free, 1)
                    pe.sem_inc(v_free, -1)
                    for k in range(2):
                        for half in range(CH):
                            t = 2 * j + k
                            last = mm(ps[:, j % 4, k * C:(k + 1) * C], X[:, half, t * 128:(t + 1) * 128],
                                      wqkv_s[:, half, 2 * C:3 * C], start=(half == 0), stop=(half == CH - 1))
                    last.then_inc(v_ready, 1)
                pe.drain().then_inc(arrived, 1)
                pe.wait_ge(go_pe, 1)
                pe.sem_inc(go_pe, -1)
                with pe.Fori(0, NHEAD // 2) as pair:
                    pe.wait_ge(wqk_ready, 2)
                    pe.sem_inc(wqk_ready, -2)
                    with pe.Fori(0, NCH // 2) as n2:
                        for p in range(2):
                            for qk in range(2):
                                pe.wait_ge((q_free, k_free)[qk], 1)
                                pe.sem_inc((q_free, k_free)[qk], -1)
                                for half in range(CH):
                                    last = mm(ps[:, 2 * p + qk, :],
                                              WQK[:, qk, half, :],
                                              X[:, half, chunk(2 * n2 + p)],
                                              start=(half == 0), stop=(half == CH - 1))
                                last.then_inc((q_ready, k_ready)[qk], 1)
                    pe.drain().then_inc(arrived, 1)
                    pe.wait_ge(go_pe, 1)
                    pe.sem_inc(go_pe, -1)

                    def score_tile(h, t, g):
                        pe.wait_ge(score_free, 1)
                        pe.sem_inc(score_free, -1)
                        for q, qs in enumerate((QA, QB)):
                            last = mm(ps[:, g % 2, :],
                                      qs.rearrange("p a n -> p (a n)")[:, bass.ds(t * 128 + h * PIX, 128)],
                                      KA.rearrange("p a n -> p (a n)")[:, bass.ds(h * PIX + g * CHUNK, CHUNK)], start=(q == 0), stop=(q == 1))
                        last.then_inc(score_ready, 1)

                    def values(h, p, g):
                        if g == 0:
                            pe.wait_ge(out_free, 1)
                            pe.sem_inc(out_free, -1)
                        pe.wait_ge(p2_ready, 1)
                        pe.sem_inc(p2_ready, -1)
                        for k in range(4):
                            j = 4 * g + k
                            for q, part in enumerate((P1, P2)):
                                last = mm(ps[:, 6 + p, 0:2 * D], part[:, g % 4, k * 128:(k + 1) * 128],
                                          V[:, bass.ds(j * NHEAD + 2 * pair + h, 1), :, :].rearrange("p o a d -> p (o a d)"),
                                          start=(j == 0 and q == 0), stop=(j == NT - 1 and q == 1))
                        if g == 7:
                            last.then_inc(out_ready, 1)

                    def slot(h, p, before, ahead):
                        for g in range(8):
                            if g % 2 == 0:
                                pe.wait_ge(prob_ready, 1)
                                pe.sem_inc(prob_ready, -1)
                            for k in range(4):
                                last = tr(ps[:, 2 + g % 4, k * 128:(k + 1) * 128],
                                          S[p][:, (4 * g + k) * 128:(4 * g + k + 1) * 128], ident_s[:, :])
                            last.then_inc(tr_ready, 1)
                            if ahead is not None:
                                score_tile(ahead[0], ahead[1], g)
                            if g >= 2:
                                values(h, p, g - 2)
                            elif before is not None:
                                values(before, 1 - p, g + 6)

                    for t in range(2):
                        for g in range(8):
                            score_tile(0, t, g)
                    for h in range(2):
                        slot(h, 0, before=0 if h == 1 else None, ahead=(h, 2))
                        with pe.Fori(0, NT // 2 - 2) as t2:
                            slot(h, 1, before=h, ahead=(h, 2 * t2 + 3))
                            slot(h, 0, before=h, ahead=(h, 2 * t2 + 4))
                        slot(h, 1, before=h, ahead=(h, NT - 1))
                        slot(h, 0, before=h, ahead=(1, 0) if h == 0 else None)
                        slot(h, 1, before=h, ahead=(1, 1) if h == 0 else None)
                    values(1, 1, 6)
                    values(1, 1, 7)
                    pe.drain().then_inc(arrived, 1)
                    pe.wait_ge(go_pe, 1)
                    pe.sem_inc(go_pe, -1)
                with pe.Fori(0, NCH // 2) as n2:
                    for p in range(2):
                        pe.wait_ge(aol_ready[p], 32)
                        pe.sem_inc(aol_ready[p], -32)
                        for half in range(CH):
                            for t in range(4):
                                last = tr(ps[:, half, t * 128:(t + 1) * 128],
                                          AOL[p][:, t, half * 128:(half + 1) * 128], ident_s[:, :])
                            last.then_inc((at_ps0, at_ps1)[half], 1)
                        pe.wait_ge(at_ready0, 1)
                        pe.sem_inc(at_ready0, -1)
                        pe.wait_ge(at_ready1, 1)
                        pe.sem_inc(at_ready1, -1)
                        for oh in range(CH):
                            pe.wait_ge(proj_free, 1)
                            pe.sem_inc(proj_free, -1)
                            for half in range(CH):
                                mm(ps[:, 2 + oh, :], wproj_s[:, half, oh * 128:(oh + 1) * 128], AT[:, half, :],
                                   start=(half == 0), stop=False)
                            for k in range(2):
                                last = mm(ps[:, 2 + oh, k * C:(k + 1) * C], POSL[p][:, k, oh * 128:(oh + 1) * 128],
                                          pos_r_s[:, :], start=False, stop=(k == 1))
                            last.then_inc(proj_ready, 1)
                pe.drain().then_inc(arrived, 1)
                pe.wait_ge(go_pe, 1)
                pe.sem_inc(go_pe, -1)
                pe.drain().then_inc(arrived, 1)
                pe.wait_ge(go_pe, 1)
                pe.sem_inc(go_pe, -1)
                def conv1(n):
                    pe.wait_ge(h1_free, 1)
                    pe.sem_inc(h1_free, -1)
                    for half in range(CH):
                        last = mm(ps[0:CB, 0, :], w1_s[:, half, :], X[:, half, chunk(n)],
                                  start=(half == 0), stop=(half == CH - 1))
                    last.then_inc(h1_ready, 1)

                def table2(n, p):
                    pe.wait_ge(stage_ready, 1)
                    pe.sem_inc(stage_ready, -1)
                    pe.wait_ge(tp_free, 1)
                    pe.sem_inc(tp_free, -1)
                    for t in range(4):
                        last = tr(ps[:, 1, t * CB:(t + 1) * CB], STG2[p][:, t * 128:(t + 1) * 128],
                                  ident_s[0:CB, 0:CB])
                    last.then_inc(tp_ready, 1)
                    if not isinstance(n, int) or n < NCH - 1:
                        conv1(n + 1)

                conv1(0)
                offset_conv(table2, lambda half: HP2, 1, PW2, 3, lambda half, ky: woff_s[:, ky, :], T2, O2, sel2_s)
                pe.drain().then_inc(arrived, 1)
                pe.wait_ge(go_pe, 1)
                pe.sem_inc(go_pe, -1)
                pe.drain().then_inc(arrived, 1)
                pe.wait_ge(go_pe, 1)
                pe.sem_inc(go_pe, -1)
                with pe.Fori(0, NT // 2) as t2:
                    for p in range(2):
                        pe.wait_ge(sm_ready, 1)
                        pe.sem_inc(sm_ready, -1)
                        for i in range(5):
                            last = tr(psf[:, i * 128:(i + 1) * 128], SM2[p][:, i * 128:(i + 1) * 128],
                                      ident_s[:, :])
                        last.then_inc(smt_ps, 1)
                        pe.wait_ge(smt_ready, 1)
                        pe.sem_inc(smt_ready, -1)
                        for i in range(5):
                            last = mm(ps[0:CB, 2, 0:128], w2_s[:, i, :], SMT2[p][:, i, :],
                                      start=(i == 0), stop=(i == 4))
                        last.then_inc(d_ready, 1)
                        pe.wait_ge(h2_ready, 1)
                        pe.sem_inc(h2_ready, -1)
                        pe.wait_ge(e_free, 1)
                        pe.sem_inc(e_free, -1)
                        for oh in range(CH):
                            last = mm(ps[:, 3 + p, oh * 128:(oh + 1) * 128], w3_s[:, oh * 128:(oh + 1) * 128],
                                      H2[p], start=True, stop=True)
                        last.then_inc(e_ready, 1)
                pe.drain().then_inc(arrived, 1)
                pe.wait_ge(go_pe, 1)
                pe.sem_inc(go_pe, -1)
                pe.drain().then_inc(arrived, 1)
                pe.wait_ge(go_pe, 1)
                pe.sem_inc(go_pe, -1)
                for layer in range(2):
                    gn_means(mean8_s)
                    pe.drain().then_inc(arrived, 1)
                    pe.wait_ge(go_pe, 1)
                    pe.sem_inc(go_pe, -1)
                    def table3(n, p):
                        pe.wait_ge(stage_ready, 2)
                        pe.sem_inc(stage_ready, -2)
                        pe.wait_ge(tp_free, 1)
                        pe.sem_inc(tp_free, -1)
                        for t in range(4):
                            for half in range(CH):
                                last = tr(psf[:, t * C + half * 128:t * C + (half + 1) * 128],
                                          STG3[p][:, half, t * 128:(t + 1) * 128], ident_s[:, :])
                        last.then_inc(tp_ready, 1)

                    offset_conv(table3, lambda half: HP7[:, half, :], CH, PW7, 7,
                                lambda half, ky: WO[:, half, ky, :], T3, O3, sel3_s)
                    pe.drain().then_inc(arrived, 1)
                    pe.wait_ge(go_pe, 1)
                    pe.sem_inc(go_pe, -1)
                    pe.drain().then_inc(arrived, 1)
                    pe.wait_ge(go_pe, 1)
                    pe.sem_inc(go_pe, -1)
                    with pe.Fori(0, NCH // 2) as g2:
                        for p in range(2):
                            pe.wait_ge(o_free, 2)
                            pe.sem_inc(o_free, -2)

                            def tap(k):
                                par = (KK * p + k) % 2
                                pe.wait_ge(st_ready, CH)
                                pe.sem_inc(st_ready, -CH)
                                for oh in range(CH):
                                    for half in range(CH):
                                        last = mm(ps[:, 4 + 2 * p + oh, :],
                                                  WD[:, k, half, oh * 128:(oh + 1) * 128], ST[par][:, half, :],
                                                  start=(k == 0 and half == 0), stop=(k == KK - 1 and half == CH - 1))
                                    if k == KK - 1:
                                        last.then_inc(o_ready, 1)
                                if k < KK - 1:
                                    last.then_inc(st_free, 1)

                            for k in range(KK):
                                par = (KK * p + k) % 2
                                for half in range(CH):
                                    for t in range(4):
                                        if half == 0:
                                            pe.wait_ge(samp_ready, 1)
                                            pe.sem_inc(samp_ready, -1)
                                            pe.sem_inc(g_free, 1)
                                        last = tr(ps[:, 2 * par + half, t * 128:(t + 1) * 128],
                                                  SAMP[par][:, t, half * 128:(half + 1) * 128], ident_s[:, :])
                                    last.then_inc(st_ps, 1)
                                if k > 0:
                                    tap(k - 1)
                            tap(KK - 1)
                    pe.drain().then_inc(arrived, 1)
                    pe.wait_ge(go_pe, 1)
                    pe.sem_inc(go_pe, -1)

        @block.scalar
        def _(act):
            af = nc.scalar.activation
            act.drain().then_inc(arrived, 1)
            act.wait_ge(go_act, 1)
            act.sem_inc(go_act, -1)

            def normed_chunks(norm):
                norm(0, 0)
                norm(1, 1)
                with act.Fori(0, NCH // 2 - 1) as n2:
                    for p in range(2):
                        norm(2 * n2 + 2 + p, p)
                act.sem_inc(image_ready, 1)

            with act.Fori(0, B) as b:
                act.wait_ge(scalar_in, 1)
                act.sem_inc(scalar_in, -1)
                af(X[:, 1, :], X[:, 1, :], ACT.Identity, scale=gsc[:, 1:2], bias=gbi[:, 1:2]).then_inc(act_step, 1)
                act.wait_ge(act_step, 1)
                act.sem_inc(act_step, -1)
                act.drain().then_inc(arrived, 1)
                act.wait_ge(go_act, 1)
                act.sem_inc(go_act, -1)
                for j in range(NT // 2):
                    act.wait_ge(v_ready, 1)
                    act.sem_inc(v_ready, -1)
                    af(V[:, 2 * j * NHEAD:2 * (j + 1) * NHEAD, 0, :],
                           ps[:, j % 4, :].rearrange("p (a d) -> p a d", d=D), ACT.Copy, scale=V_SCALE).then_inc(v1_done, 1)
                act.drain().then_inc(arrived, 1)
                act.wait_ge(go_act, 1)
                act.sem_inc(go_act, -1)
                with act.Fori(0, NHEAD // 2) as pair:
                    with act.Fori(0, NCH // 2) as n2:
                        for p in range(2):
                            n = 2 * n2 + p
                            at = chunk(n)
                            act.wait_ge(q_ready, 1)
                            act.sem_inc(q_ready, -1)
                            af(QA[0:64, 0, at], ps[0:64, 2 * p, :], ACT.Copy, scale=QK_SCALE)
                            af(QA[64:128, 1, at], ps[64:128, 2 * p, :], ACT.Copy, scale=QK_SCALE).then_inc(qa_done, 1)
                            act.wait_ge(k_ready, 1)
                            act.sem_inc(k_ready, -1)
                            act.wait_ge(kt_free[p], 32)
                            act.sem_inc(kt_free[p], -32)
                            af(KA[0:64, 0, at], ps[0:64, 2 * p + 1, :], ACT.Copy, scale=QK_SCALE)
                            af(KT[p][64:128], ps[64:128, 2 * p + 1, :], ACT.Copy, scale=QK_SCALE).then_inc(ka_done, 1)
                    act.drain().then_inc(arrived, 1)
                    act.wait_ge(go_act, 1)
                    act.sem_inc(go_act, -1)

                    def softmax(p, i):
                        if i == 0:
                            act.wait_ge(max_ready, 1)
                            act.sem_inc(max_ready, -1)
                        at = slice(i * 1024, (i + 1) * 1024)
                        af(S[p][:, at], S[p][:, at], ACT.Exp, bias=nmx[p], accum_out=rs[p][:, i:i + 1]).then_inc(prob_ready, 1)

                    def slot(p, before=True, ahead=True):
                        for g in range(8):
                            act.wait_ge(tr_ready, 1)
                            act.sem_inc(tr_ready, -1)
                            af(P1[:, g % 4, :], ps[:, 2 + g % 4, :], ACT.Copy).then_inc(p1_ready, 1)
                            if ahead and g % 2 == 0:
                                softmax(1 - p, g // 2)
                            if before and g == 3:
                                output(1 - p)

                    def output(p):
                        act.wait_ge(rr_ready, 1)
                        act.sem_inc(rr_ready, -1)
                        act.wait_ge(out_ready, 1)
                        act.sem_inc(out_ready, -1)
                        af(O1[p].rearrange("p a d -> p (a d)"), ps[:, 6 + p, 0:2 * D], ACT.Copy, scale=rr[p]).then_inc(o1_ready, 1)

                    for i in range(4):
                        softmax(0, i)
                    slot(0, before=False)
                    with act.Fori(0, NT - 1) as t2:
                        slot(1)
                        slot(0)
                    slot(1, ahead=False)
                    output(1)
                    act.drain().then_inc(arrived, 1)
                    act.wait_ge(go_act, 1)
                    act.sem_inc(go_act, -1)
                with act.Fori(0, NCH // 2) as n2:
                    for p in range(2):
                        act.wait_ge(at_ps1, 1)
                        act.sem_inc(at_ps1, -1)
                        af(AT[:, 1, :], ps[:, 1, :], ACT.Copy).then_inc(at_ready1, 1)
                act.drain().then_inc(arrived, 1)
                act.wait_ge(go_act, 1)
                act.sem_inc(go_act, -1)
                act.drain().then_inc(arrived, 1)
                act.wait_ge(go_act, 1)
                act.sem_inc(go_act, -1)
                def norm2(n, p):
                    act.wait_ge(h1_ready, 1)
                    act.sem_inc(h1_ready, -1)
                    act.wait_ge(stage_free, 1)
                    act.sem_inc(stage_free, -1)
                    af(STG2[p], ps[0:CB, 0, :], ACT.Relu, scale=bnf[:, 0:1], bias=bnf[:, 1:2]).then_inc(stage_ready, 1)
                    af(HP2.rearrange("p (y x) -> p y x", y=PW2)[:, bass.ds(8 * n + 1, 8), 1:1 + W],
                            ps[0:CB, 0, :].rearrange("p (y x) -> p y x", x=W), ACT.Relu,
                            scale=bnf[:, 0:1], bias=bnf[:, 1:2]).then_inc(act_step, 1)
                    act.wait_ge(act_step, 1)
                    act.sem_inc(act_step, -1)
                    act.sem_inc(h1_free, 1)
                    if not isinstance(n, int) or n > 0:
                        act.sem_inc(image_ready, 1)

                normed_chunks(norm2)
                act.drain().then_inc(arrived, 1)
                act.wait_ge(go_act, 1)
                act.sem_inc(go_act, -1)
                af(MASK2, OFF2[:, :, O3:O2], ACT.Sigmoid).then_inc(mask_ready, 1)
                act.drain().then_inc(arrived, 1)
                act.wait_ge(go_act, 1)
                act.sem_inc(go_act, -1)
                with act.Fori(0, NT // 2) as t2:
                    for p in range(2):
                        act.wait_ge(smt_ps, 1)
                        act.sem_inc(smt_ps, -1)
                        act.sem_inc(sm_free, 1)
                        af(SMT2[p].rearrange("p a b -> p (a b)"), psf[:, 0:5 * 128], ACT.Copy).then_inc(smt_ready, 1)
                        act.wait_ge(d_ready, 1)
                        act.sem_inc(d_ready, -1)
                        af(H2[p], ps[0:CB, 2, 0:128], ACT.Relu, scale=bnf[:, 2:3], bias=bnf[:, 3:4]).then_inc(h2_ready, 1)
                act.drain().then_inc(arrived, 1)
                act.wait_ge(go_act, 1)
                act.sem_inc(go_act, -1)
                af(X[:, 0, :], X[:, 0, :], ACT.Relu, bias=bn3b[:, 0:1]).then_inc(act_step, 1)
                act.wait_ge(act_step, 1)
                act.sem_inc(act_step, -1)
                act.drain().then_inc(arrived, 1)
                act.wait_ge(go_act, 1)
                act.sem_inc(go_act, -1)
                for layer in range(2):
                    src = X[:, :, :] if layer == 0 else OUT
                    act.drain().then_inc(arrived, 1)
                    act.wait_ge(go_act, 1)
                    act.sem_inc(go_act, -1)
                    def norm3(n, p):
                        act.wait_ge(stage_free, 1)
                        act.sem_inc(stage_free, -1)
                        for half in range(CH):
                            af(STG3[p][:, half, :], src[:, half, chunk(n)], ACT.Relu,
                                   scale=gsc[:, half:half + 1], bias=gbi[:, half:half + 1]).then_inc(stage_ready, 1)
                        for half in range(CH):
                            padded = HP7[:, half, :].rearrange("p (y x) -> p y x", y=PW7)
                            af(padded[:, bass.ds(8 * n + 3, 8), 3:3 + W],
                                   src[:, half, chunk(n)].rearrange("p (y x) -> p y x", x=W), ACT.Relu,
                                   scale=gsc[:, half:half + 1], bias=gbi[:, half:half + 1]).then_inc(act_step, 1)
                        act.wait_ge(act_step, 2)
                        act.sem_inc(act_step, -2)
                        if not isinstance(n, int) or n > 0:
                            act.sem_inc(image_ready, 1)

                    normed_chunks(norm3)
                    act.drain().then_inc(arrived, 1)
                    act.wait_ge(go_act, 1)
                    act.sem_inc(go_act, -1)
                    act.drain().then_inc(arrived, 1)
                    act.wait_ge(go_act, 1)
                    act.sem_inc(go_act, -1)
                    def product(g2, i):
                        p, k = divmod(i, KK)
                        uses = (2 * g2 + p + (2 * b + layer) * NCH) * 3 + k // 3 + 1
                        act.wait_ge(g_ready[k % 3], uses * 16 * 4)
                        act.sem_inc(gathers_seen, 1)
                        for t in range(4):
                            wcol = (t * KK + k) * 4
                            af(SAMP[i % 2][:, t, :], G3[4 * (k % 3) + t][:, 0, :], ACT.Copy,
                                   scale=WS3[p][:, wcol:wcol + 1]).then_inc(prod_ready, 1)

                    def output(g2, p):
                        for oh in range(CH):
                            act.wait_ge(o_ready, 1)
                            act.sem_inc(o_ready, -1)
                            if oh == CH - 1:
                                act.sem_inc(st_free, 1)
                            af(OUT[:, oh, chunk(2 * g2 + p)], ps[:, 4 + 2 * p + oh, :], ACT.Identity,
                                    bias=vec_s[:, (B1, B2)[layer], oh:oh + 1]).then_inc(act_step, 1)
                            act.wait_ge(act_step, 1)
                            act.sem_inc(act_step, -1)
                            act.sem_inc(o_free, 1)
                            if layer == 1:
                                act.sem_inc(out_filled, 1)

                    def pair(g2, last):
                        for i in range(2 * KK):
                            if i + 1 < 2 * KK:
                                product(g2, i + 1)
                            elif not last:
                                product(g2 + 1, 0)
                            if i == KK:
                                output(g2, 0)
                            act.wait_ge(st_free, 1)
                            act.sem_inc(st_free, -1)
                            for half in range(CH):
                                act.wait_ge(st_ps, 1)
                                act.sem_inc(st_ps, -1)
                                af(ST[i % 2][:, half, :], ps[:, 2 * (i % 2) + half, :], ACT.Copy).then_inc(st_ready, 1)
                        output(g2, 1)

                    product(0, 0)
                    with act.Fori(0, NCH // 2 - 1) as g2:
                        pair(g2, False)
                    pair(NCH // 2 - 1, True)
                    act.drain().then_inc(arrived, 1)
                    act.wait_ge(go_act, 1)
                    act.sem_inc(go_act, -1)

        @block.vector
        def _(dve):
            v = nc.vector
            dve.sem_inc(v_free, 4)
            dve.sem_inc(q_free, 2)
            dve.sem_inc(k_free, 2)
            dve.sem_inc(score_free, 2)
            dve.sem_inc(out_free, 2)
            dve.sem_inc(ao_free0, 16)
            dve.sem_inc(kt_free0, 32)
            dve.sem_inc(kt_free1, 32)
            dve.sem_inc(ao_free1, 16)
            dve.sem_inc(aol_free, 2)
            dve.sem_inc(proj_free, 2)
            dve.sem_inc(h1_free, 1)
            dve.sem_inc(stage_free, 2)
            dve.sem_inc(tp_free, 1)
            dve.sem_inc(ts_free0, 128)
            dve.sem_inc(ts_free1, 128)
            dve.sem_inc(off_free, 2)
            dve.sem_inc(g2_free, 2)
            dve.sem_inc(sm_free, 2)
            dve.sem_inc(e_free, 2)
            dve.sem_inc(g_free, NG)
            dve.sem_inc(st_free, 2)
            dve.sem_inc(o_free, 4)
            dve.drain().then_inc(arrived, 1)
            dve.wait_ge(go_dve, 1)
            dve.sem_inc(go_dve, -1)


            def fold(sc, bi, g, bb, m, var, extra=None):
                v.tensor_scalar(sc, var, EPS, None, ALU.add).then_inc(dve_step, 1)
                dve.wait_ge(dve_step, 1)
                dve.sem_inc(dve_step, -1)
                dve.sem_inc(root_in, 1)
                dve.wait_ge(root_ready, 1)
                dve.sem_inc(root_ready, -1)
                v.tensor_tensor(sc, sc, g, ALU.mult).then_inc(dve_step, 1)
                dve.wait_ge(dve_step, 1)
                dve.sem_inc(dve_step, -1)
                if extra is None:
                    v.tensor_tensor(bi, m, sc, ALU.mult).then_inc(dve_step, 1)
                    dve.wait_ge(dve_step, 1)
                    dve.sem_inc(dve_step, -1)
                    v.tensor_tensor(bi, bb, bi, ALU.subtract).then_inc(dve_step, 1)
                    dve.wait_ge(dve_step, 1)
                    dve.sem_inc(dve_step, -1)
                else:
                    v.tensor_tensor(bi, extra, m, ALU.subtract).then_inc(dve_step, 1)
                    dve.wait_ge(dve_step, 1)
                    dve.sem_inc(dve_step, -1)
                    v.tensor_tensor(bi, bi, sc, ALU.mult).then_inc(dve_step, 1)
                    dve.wait_ge(dve_step, 1)
                    dve.sem_inc(dve_step, -1)
                    v.tensor_tensor(bi, bi, bb, ALU.add).then_inc(dve_step, 1)
                    dve.wait_ge(dve_step, 1)
                    dve.sem_inc(dve_step, -1)

            def col(i):
                return vec64_s[:, i:i + 1]
            fold(bnf[:, 0:1], bnf[:, 1:2], col(BN1_G), col(BN1_B), col(BN1_M), col(BN1_V))
            fold(bnf[:, 2:3], bnf[:, 3:4], col(BN2_G), col(BN2_B), col(BN2_M), col(BN2_V), col(DCN_B))
            fold(bn3s[:, :], bn3b[:, :], vec_s[:, BN3_G, :], vec_s[:, BN3_B, :], vec_s[:, BN3_M, :],
                 vec_s[:, BN3_V, :])

            def group_norm(src, gamma, beta):
                for half in range(CH):
                    for c in range(8):
                        last = v.bn_stats(bnst[:, half, c, :], src[:, half, c * 512:(c + 1) * 512])
                last.then_inc(dve_step, 1)
                dve.wait_ge(dve_step, 1)
                dve.sem_inc(dve_step, -1)
                for half in range(CH):
                    last = v.bn_aggr(mv[:, half, :], bnst[:, half, :, :].rearrange("p a b -> p (a b)"))
                last.then_inc(dve_step, 1)
                dve.wait_ge(dve_step, 1)
                dve.sem_inc(dve_step, -1)
                v.tensor_tensor(gsq[:, :], mv[:, :, 0], mv[:, :, 0], ALU.mult).then_inc(dve_step, 1)
                dve.wait_ge(dve_step, 1)
                dve.sem_inc(dve_step, -1)
                v.tensor_tensor(mv[:, :, 1], mv[:, :, 1], gsq[:, :], ALU.add).then_inc(dve_step, 1)
                dve.wait_ge(dve_step, 1)
                dve.sem_inc(dve_step, -1)
                dve.sem_inc(gn_stat, 1)
                dve.wait_ge(gn_mean, 1)
                dve.sem_inc(gn_mean, -1)
                v.tensor_copy(gm[:, :, :].rearrange("p a b -> p (a b)"), ps[:, 7, 0:2 * CH]).then_inc(dve_step, 1)
                dve.wait_ge(dve_step, 1)
                dve.sem_inc(dve_step, -1)
                v.tensor_tensor(gsq[:, :], gm[:, :, 0], gm[:, :, 0], ALU.mult).then_inc(dve_step, 1)
                dve.wait_ge(dve_step, 1)
                dve.sem_inc(dve_step, -1)
                v.tensor_tensor(gvar[:, :], gm[:, :, 1], gsq[:, :], ALU.subtract).then_inc(dve_step, 1)
                dve.wait_ge(dve_step, 1)
                dve.sem_inc(dve_step, -1)
                v.tensor_scalar(grs[:, :], gvar[:, :], EPS, None, ALU.add).then_inc(dve_step, 1)
                dve.wait_ge(dve_step, 1)
                dve.sem_inc(dve_step, -1)
                dve.sem_inc(root_in, 1)
                dve.wait_ge(root_ready, 1)
                dve.sem_inc(root_ready, -1)
                v.tensor_tensor(gsc[:, :], grs[:, :], vec_s[:, gamma, :], ALU.mult).then_inc(dve_step, 1)
                dve.wait_ge(dve_step, 1)
                dve.sem_inc(dve_step, -1)
                v.tensor_tensor(gtm[:, :], gm[:, :, 0], gsc[:, :], ALU.mult).then_inc(dve_step, 1)
                dve.wait_ge(dve_step, 1)
                dve.sem_inc(dve_step, -1)
                v.tensor_tensor(gbi[:, :], vec_s[:, beta, :], gtm[:, :], ALU.subtract).then_inc(dve_step, 1)
                dve.wait_ge(dve_step, 1)
                dve.sem_inc(dve_step, -1)

            def table_and_offsets(stage, pv, off, base, ksize, pw_, tbuf, sel, no):
                def tiles(p):
                    dve.wait_ge(tp_ready, 1)
                    dve.sem_inc(tp_ready, -1)
                    dve.wait_ge(ts_free[p], 16 * 8)
                    dve.sem_inc(ts_free[p], -16 * 8)
                    v.tensor_copy(stage[p].rearrange("p a b -> p (a b)"), pv).then_inc(dve_step, 1)
                    dve.wait_ge(dve_step, 1)
                    dve.sem_inc(dve_step, -1)
                    dve.sem_inc(tp_free, 1)
                    dve.sem_inc(ts_ready, 1)
                    dve.sem_inc(stage_free, 1)

                def block(blk, p):
                    for kx in range(ksize):
                        for j in range(2):
                            if kx == 0:
                                dve.wait_ge(t_ps, 1)
                                dve.sem_inc(t_ps, -1)
                            else:
                                dve.wait_ge(chain, 2 * (kx - 1) + j + 1)
                            moved = ps[0:ksize * no, 2 + 2 * p + j, 0:4 * pw_].rearrange(
                                "q (y x) -> q y x", x=pw_)[:, :, kx:kx + W]
                            rows = tbuf[p][:, j * 4 * W:(j + 1) * 4 * W].rearrange("q (y x) -> q y x", x=W)
                            if kx == 0:
                                ins = v.tensor_scalar(rows, moved, sel[:, kx:kx + 1], None, ALU.mult)
                            else:
                                ins = v.scalar_tensor_tensor(rows, moved, sel[:, kx:kx + 1], rows,
                                                             op0=ALU.mult, op1=ALU.add)
                            ins.then_inc(chain if kx < ksize - 1 else t_ready, 1)
                    dve.sem_inc(chain, -2 * (ksize - 1))
                    at = bass.ds(blk * 4 * no, 4 * no)
                    dve.wait_ge(off_ready, 1)
                    dve.sem_inc(off_ready, -1)
                    v.tensor_tensor(off.rearrange("p a b -> p (a b)")[:, at], ps[:, 6 + p, 0:4 * no],
                                        base.rearrange("p a b -> p (a b)")[:, at], ALU.add).then_inc(off_free, 1)

                tiles(0)
                tiles(1)
                with dve.Fori(0, NCH // 2 - 1) as n2:
                    for p in range(2):
                        tiles(p)
                        block(2 * n2 + p, p)
                for p in range(2):
                    block(NCH - 2 + p, p)

            def corners(off, co, fr, w4, idx, mask=None):
                v.tensor_scalar(co, off[:, :, 0:O3], 0.0, float(H + 1), ALU.max, ALU.min).then_inc(dve_step, 1)
                dve.wait_ge(dve_step, 1)
                dve.sem_inc(dve_step, -1)
                fl = w4.rearrange("p a k c -> p a (k c)")[:, :, 0:O3]
                whole = fr.bitcast(I32)
                v.tensor_copy(whole, co).then_inc(dve_step, 1)
                dve.wait_ge(dve_step, 1)
                dve.sem_inc(dve_step, -1)
                v.tensor_copy(fl, whole).then_inc(dve_step, 1)
                dve.wait_ge(dve_step, 1)
                dve.sem_inc(dve_step, -1)
                v.tensor_tensor(fr, fl, co, ALU.is_gt).then_inc(dve_step, 1)
                dve.wait_ge(dve_step, 1)
                dve.sem_inc(dve_step, -1)
                v.tensor_tensor(fl, fl, fr, ALU.subtract).then_inc(dve_step, 1)
                dve.wait_ge(dve_step, 1)
                dve.sem_inc(dve_step, -1)
                v.tensor_tensor(fr, co, fl, ALU.subtract).then_inc(dve_step, 1)
                dve.wait_ge(dve_step, 1)
                dve.sem_inc(dve_step, -1)
                fl2 = fl.rearrange("p a (k two) -> p a k two", two=2)
                cy = co.rearrange("p a (k two) -> p a k two", two=2)
                fy = fr.rearrange("p a (k two) -> p a k two", two=2)
                v.scalar_tensor_tensor(co[:, :, 0:KK], fl2[:, :, :, 0], float(TY), fl2[:, :, :, 1],
                                            op0=ALU.mult, op1=ALU.add).then_inc(dve_step, 1)
                dve.wait_ge(dve_step, 1)
                dve.sem_inc(dve_step, -1)
                v.tensor_copy(idx, co[:, :, 0:KK]).then_inc(dve_step, 1)
                dve.wait_ge(dve_step, 1)
                dve.sem_inc(dve_step, -1)
                v.tensor_scalar(co, fr, -1.0, 1.0, ALU.mult, ALU.add).then_inc(dve_step, 1)
                dve.wait_ge(dve_step, 1)
                dve.sem_inc(dve_step, -1)
                if mask is not None:
                    dve.wait_ge(mask_ready, 1)
                    dve.sem_inc(mask_ready, -1)
                    for part in (cy, fy):
                        v.tensor_tensor(part[:, :, :, 0], part[:, :, :, 0], mask, ALU.mult).then_inc(dve_step, 1)
                        dve.wait_ge(dve_step, 1)
                        dve.sem_inc(dve_step, -1)
                v.tensor_tensor(w4[:, :, :, 0], cy[:, :, :, 0], cy[:, :, :, 1], ALU.mult).then_inc(dve_step, 1)
                dve.wait_ge(dve_step, 1)
                dve.sem_inc(dve_step, -1)
                v.tensor_tensor(w4[:, :, :, 1], cy[:, :, :, 0], fy[:, :, :, 1], ALU.mult).then_inc(dve_step, 1)
                dve.wait_ge(dve_step, 1)
                dve.sem_inc(dve_step, -1)
                v.tensor_tensor(w4[:, :, :, 2], fy[:, :, :, 0], cy[:, :, :, 1], ALU.mult).then_inc(dve_step, 1)
                dve.wait_ge(dve_step, 1)
                dve.sem_inc(dve_step, -1)
                v.tensor_tensor(w4[:, :, :, 3], fy[:, :, :, 0], fy[:, :, :, 1], ALU.mult).then_inc(dve_step, 1)
                dve.wait_ge(dve_step, 1)
                dve.sem_inc(dve_step, -1)

            with dve.Fori(0, B) as b:
                dve.wait_ge(x_loaded, 16)
                dve.sem_inc(x_loaded, -16)
                group_norm(X[:, :, :], GN0_G, GN0_B)
                dve.sem_inc(scalar_in, 1)
                v.tensor_scalar(X[:, 0, :], X[:, 0, :], gsc[:, 0:1], gbi[:, 0:1], ALU.mult, ALU.add).then_inc(dve_step, 1)
                dve.wait_ge(dve_step, 1)
                dve.sem_inc(dve_step, -1)
                dve.drain().then_inc(arrived, 1)
                dve.wait_ge(go_dve, 1)
                dve.sem_inc(go_dve, -1)
                for j in range(NT // 2):
                    dve.wait_ge(v1_done, 1)
                    dve.sem_inc(v1_done, -1)
                    at = slice(2 * j * NHEAD, 2 * (j + 1) * NHEAD)
                    v.scalar_tensor_tensor(V[:, at, 1, :], ps[:, j % 4, :].rearrange("p (a d) -> p a d", d=D),
                                               V_SCALE, V[:, at, 0, :], op0=ALU.mult, op1=ALU.subtract).then_inc(v_free, 1)
                dve.drain().then_inc(arrived, 1)
                dve.wait_ge(go_dve, 1)
                dve.sem_inc(go_dve, -1)
                with dve.Fori(0, NHEAD // 2) as pair:
                    with dve.Fori(0, NCH // 2) as n2:
                        for p in range(2):
                            at = chunk(2 * n2 + p)
                            dve.wait_ge(qa_done, 1)
                            dve.sem_inc(qa_done, -1)
                            for hh in range(2):
                                part = slice(64 * hh, 64 * (hh + 1))
                                last = v.scalar_tensor_tensor(QB[part, hh, at], ps[part, 2 * p, :], QK_SCALE,
                                                              QA[part, hh, at], op0=ALU.mult, op1=ALU.subtract)
                            last.then_inc(q_free, 1)
                            dve.wait_ge(ka_done, 1)
                            dve.sem_inc(ka_done, -1)
                            v.scalar_tensor_tensor(KT[p][0:64], ps[0:64, 2 * p + 1, :], QK_SCALE, KA[0:64, 0, at],
                                                   op0=ALU.mult, op1=ALU.subtract)
                            v.scalar_tensor_tensor(KA[64:128, 1, at], ps[64:128, 2 * p + 1, :], QK_SCALE,
                                                        KT[p][64:128], op0=ALU.mult, op1=ALU.subtract).then_inc(dve_step, 1)
                            dve.wait_ge(dve_step, 1)
                            dve.sem_inc(dve_step, -1)
                            dve.sem_inc(k_free, 1)
                            dve.sem_inc(dup_ready, 1)
                    dve.drain().then_inc(arrived, 1)
                    dve.wait_ge(go_dve, 1)
                    dve.sem_inc(go_dve, -1)

                    def score_in(p, g):
                        dve.wait_ge(score_ready, 1)
                        dve.sem_inc(score_ready, -1)
                        v.tensor_scalar(S[p][:, g * CHUNK:(g + 1) * CHUNK], ps[:, g % 2, :],
                                            float(D) ** -0.5 / QK_SCALE ** 2, -3.0e38, ALU.mult, ALU.max,
                                            accum_out=mx[p][:, g:g + 1]).then_inc(score_free if g < 7 else row_done, 1)

                    def maximum(p):
                        dve.wait_ge(row_done, 1)
                        dve.sem_inc(row_done, -1)
                        dve.sem_inc(score_free, 1)
                        v.tensor_reduce(nmx[p], mx[p], AX.X, ALU.max, negate=True).then_inc(dve_step, 1)
                        dve.wait_ge(dve_step, 1)
                        dve.sem_inc(dve_step, -1)
                        v.tensor_scalar(nmx[p], nmx[p], LN_P_MAX, None, ALU.add).then_inc(max_ready, 1)

                    def slot(p, ahead=True):
                        for g in range(8):
                            if ahead:
                                score_in(p, g)
                            dve.wait_ge(p1_ready, 1)
                            dve.sem_inc(p1_ready, -1)
                            v.tensor_tensor(P2[:, g % 4, :], ps[:, 2 + g % 4, :], P1[:, g % 4, :], ALU.subtract).then_inc(p2_ready, 1)
                        v.tensor_reduce(rsum[p], rs[p], AX.X, ALU.add).then_inc(dve_step, 1)
                        dve.wait_ge(dve_step, 1)
                        dve.sem_inc(dve_step, -1)
                        v.reciprocal(rr[p], rsum[p]).then_inc(rr_ready, 1)
                        if ahead:
                            maximum(p)

                    for p in range(2):
                        for g in range(8):
                            score_in(p, g)
                        maximum(p)
                    with dve.Fori(0, NT - 1) as t2:
                        slot(0)
                        slot(1)
                    slot(0, ahead=False)
                    slot(1, ahead=False)
                    dve.drain().then_inc(arrived, 1)
                    dve.wait_ge(go_dve, 1)
                    dve.sem_inc(go_dve, -1)
                with dve.Fori(0, NCH // 2) as n2:
                    for p in range(2):
                        dve.wait_ge(at_ps0, 1)
                        dve.sem_inc(at_ps0, -1)
                        v.tensor_copy(AT[:, 0, :], ps[:, 0, :]).then_inc(at_ready0, 1)
                        for oh in range(CH):
                            at = chunk(2 * n2 + p)
                            dve.wait_ge(proj_ready, 1)
                            dve.sem_inc(proj_ready, -1)
                            if oh == CH - 1:
                                dve.sem_inc(aol_free, 1)
                            v.tensor_tensor(X[:, oh, at], ps[:, 2 + oh, :], X[:, oh, at], ALU.add).then_inc(proj_free, 1)
                dve.drain().then_inc(arrived, 1)
                dve.wait_ge(go_dve, 1)
                dve.sem_inc(go_dve, -1)
                dve.wait_ge(x_loaded, 16)
                dve.sem_inc(x_loaded, -16)
                v.tensor_tensor(BASE2, BASE2, boff_s[:, :].unsqueeze(1).to_broadcast([128, NT, O2]), ALU.add).then_inc(dve_step, 1)
                dve.wait_ge(dve_step, 1)
                dve.sem_inc(dve_step, -1)
                dve.drain().then_inc(arrived, 1)
                dve.wait_ge(go_dve, 1)
                dve.sem_inc(go_dve, -1)
                table_and_offsets(TS2, ps[:, 1, 0:4 * CB], OFF2, BASE2, 3, PW2, T2, sel2_s, O2)
                dve.drain().then_inc(arrived, 1)
                dve.wait_ge(go_dve, 1)
                dve.sem_inc(go_dve, -1)
                corners(OFF2, CO2, FR2, W4_2, IDX2, MASK2)
                dve.drain().then_inc(arrived, 1)
                dve.wait_ge(go_dve, 1)
                dve.sem_inc(go_dve, -1)
                def sample(t, turn, p):
                    v.tensor_copy(WS2[p], W4_2.rearrange("p a k c -> p (a k c)")[:, bass.ds(t * KK * 4, KK * 4)]).then_inc(dve_step, 1)
                    dve.wait_ge(dve_step, 1)
                    dve.sem_inc(dve_step, -1)
                    dve.wait_ge(g2_ready[p], (b * (NT // 2) + turn + 1) * 16 * KK)
                    dve.sem_inc(gathers_seen, 1)
                    corner4 = G2[p].rearrange("p k (q c) -> p (k q) c", q=4)
                    v.tensor_tensor(corner4, corner4, WS2[p].unsqueeze(2).to_broadcast([128, KK * 4, CB]),
                                         ALU.mult).then_inc(dve_step, 1)
                    dve.wait_ge(dve_step, 1)
                    dve.sem_inc(dve_step, -1)
                    v.tensor_tensor(A2, G2[p][:, :, 0:2 * CB], G2[p][:, :, 2 * CB:4 * CB], ALU.add).then_inc(dve_step, 1)
                    dve.wait_ge(dve_step, 1)
                    dve.sem_inc(dve_step, -1)
                    dve.sem_inc(g2_free, 1)
                    dve.wait_ge(sm_free, 1)
                    dve.sem_inc(sm_free, -1)
                    v.tensor_tensor(SM2[p][:, 0:KK * CB].rearrange("p (k c) -> p k c", k=KK),
                                        A2[:, :, 0:CB], A2[:, :, CB:2 * CB], ALU.add).then_inc(sm_ready, 1)

                def residual(t, p):
                    dve.wait_ge(e_ready, 1)
                    dve.sem_inc(e_ready, -1)
                    at = bass.ds(t * 128, 128)
                    for oh in range(CH):
                        last = v.scalar_tensor_tensor(X[:, oh, at], ps[:, 3 + p, oh * 128:(oh + 1) * 128],
                                                      bn3s[:, oh:oh + 1], X[:, oh, at], op0=ALU.mult, op1=ALU.add)
                    last.then_inc(dve_step, 1)
                    dve.wait_ge(dve_step, 1)
                    dve.sem_inc(dve_step, -1)
                    dve.sem_inc(e_free, 1)

                sample(0, 0, 0)
                with dve.Fori(0, NT // 2 - 1) as t2:
                    for p in range(2):
                        sample(2 * t2 + 1 + p, t2 + p, 1 - p)
                        residual(2 * t2 + p, p)
                sample(NT - 1, NT // 2 - 1, 1)
                for p in range(2):
                    residual(NT - 2 + p, p)
                dve.drain().then_inc(arrived, 1)
                dve.wait_ge(go_dve, 1)
                dve.sem_inc(go_dve, -1)
                v.tensor_scalar(X[:, 1, :], X[:, 1, :], bn3b[:, 1:2], 0.0, ALU.add, ALU.max).then_inc(dve_step, 1)
                dve.wait_ge(dve_step, 1)
                dve.sem_inc(dve_step, -1)
                dve.drain().then_inc(arrived, 1)
                dve.wait_ge(go_dve, 1)
                dve.sem_inc(go_dve, -1)
                for layer in range(2):
                    group_norm(X[:, :, :] if layer == 0 else OUT, (GN1_G, GN2_G)[layer], (GN1_B, GN2_B)[layer])
                    for half in range(CH):
                        v.tensor_tensor(WO[:, half, :, :].rearrange("p a (b o) -> p (a b) o", o=O3),
                                             dw_s[:, layer, half, :].unsqueeze(2).to_broadcast([128, 49, O3]),
                                             pw_s[:, layer, half, :].unsqueeze(1).to_broadcast([128, 49, O3]),
                                             ALU.mult).then_inc(dve_step, 1)
                        dve.wait_ge(dve_step, 1)
                        dve.sem_inc(dve_step, -1)
                    dve.drain().then_inc(arrived, 1)
                    dve.wait_ge(go_dve, 1)
                    dve.sem_inc(go_dve, -1)
                    dve.wait_ge(wd_loaded, 32)
                    v.tensor_tensor(BASE3, BASE3, pwb_s[:, layer, :].unsqueeze(1).to_broadcast([128, NT, O3]),
                                         ALU.add).then_inc(dve_step, 1)
                    dve.wait_ge(dve_step, 1)
                    dve.sem_inc(dve_step, -1)
                    table_and_offsets(TS3, psf[:, 0:4 * C], OFF3, BASE3, 7, PW7, T3, sel3_s, O3)
                    dve.drain().then_inc(arrived, 1)
                    dve.wait_ge(go_dve, 1)
                    dve.sem_inc(go_dve, -1)
                    corners(OFF3, OFF3, FR3, W4_3, IDX3)
                    dve.drain().then_inc(arrived, 1)
                    dve.wait_ge(go_dve, 1)
                    dve.sem_inc(go_dve, -1)
                    def residual3(g):
                        for oh in range(CH):
                            dve.wait_ge(out_filled, 1)
                            dve.sem_inc(out_filled, -1)
                            v.tensor_tensor(OUT[:, oh, chunk(g)], OUT[:, oh, chunk(g)], X[:, oh, chunk(g)],
                                                ALU.add).then_inc(fo_ready, 1)

                    def pair(g2, first):
                        for p in range(2):
                            for k in range(KK):
                                par = (KK * p + k) % 2
                                for corner in range(1, 4):
                                    for t in range(4):
                                        slot = 4 * (k % 3) + t
                                        wcol = (t * KK + k) * 4 + corner
                                        sample = SAMP[par][:, t, :]
                                        if corner == 1:
                                            dve.wait_ge(prod_ready, 1)
                                            dve.sem_inc(prod_ready, -1)
                                        else:
                                            dve.wait_ge(chain, 4 * (corner - 2) + t + 1)
                                        ins = v.scalar_tensor_tensor(sample, G3[slot][:, corner, :],
                                                                     WS3[p][:, wcol:wcol + 1], sample,
                                                                     op0=ALU.mult, op1=ALU.add)
                                        ins.then_inc(chain if corner < 3 else samp_ready, 1)
                                dve.sem_inc(chain, -8)
                                if layer == 1 and k == 3 and not (first and p == 0):
                                    residual3(2 * g2 + p - 1)

                    if layer == 1:
                        pair(0, True)
                        with dve.Fori(1, NCH // 2) as g2:
                            pair(g2, False)
                        residual3(NCH - 1)
                    else:
                        with dve.Fori(0, NCH // 2) as g2:
                            pair(g2, False)
                    dve.drain().then_inc(arrived, 1)
                    dve.wait_ge(go_dve, 1)
                    dve.sem_inc(go_dve, -1)


def constants():
    ident = np.eye(128, dtype=np.float32)
    mean32 = np.kron(np.eye(4), np.full((32, 32), 1 / 32)).astype(np.float32)
    mean8 = np.kron(np.eye(16), np.full((8, 8), 1 / 8)).astype(np.float32)
    sel2 = np.zeros((3 * O2, 3 + O2), np.float32)
    sel3 = np.zeros((7 * O3, 7 + O3), np.float32)
    for sel, ks, no in ((sel2, 3, O2), (sel3, 7, O3)):
        for kx in range(ks):
            for o in range(no):
                sel[kx * no + o, [kx, ks + o]] = 1.0
    pix = np.arange(PIX).reshape(NT, 128).T
    grid = np.zeros((128, NT, KK, 2), np.float32)
    for k in range(KK):
        grid[:, :, k, 0] = pix // W - 1 + k // 3 + 1
        grid[:, :, k, 1] = pix % W - 1 + k % 3 + 1
    base3 = grid.reshape(128, NT, O3)
    base2 = np.concatenate([base3, np.zeros((128, NT, KK), np.float32)], axis=2)
    one = np.float32(1)
    jj = np.arange(W, dtype=np.float32) / np.float32(W - 1)
    ii = np.arange(H, dtype=np.float32) / np.float32(H - 1)
    at = np.arange(C)[None, :] * NPOS + np.arange(NPOS)[:, None]
    pos = np.stack([jj[at % W], ii[at // W], one - jj[at % W], one - ii[at // W], np.ones(at.shape, np.float32)])
    return ident, mean32, mean8, sel2, sel3, base2, base3, pos.astype(np.float32)


def kernel(**a):
    import concourse.bacc as bacc
    from concourse.bass_utils import run_bass_kernel_spmd

    a = {k: np.asarray(v) for k, v in a.items()}
    ident, mean32, mean8, sel2, sel3, base2, base3, pos = constants()
    halves = lambda m: np.ascontiguousarray(m.reshape(CH, 128, -1).transpose(1, 0, 2))
    vec = np.stack([a[n] for n in ("L0_conv_gn_gamma", "L0_conv_gn_beta", "L2_conv_bn3_g", "L2_conv_bn3_b",
                                   "L2_conv_bn3_m", "L2_conv_bn3_v", "L3_conv_gn1_g", "L3_conv_gn1_b", "L3_conv_b1",
                                   "L3_conv_gn2_g", "L3_conv_gn2_b", "L3_conv_b2")])
    vec64 = np.stack([a["L2_conv_" + n] for n in ("bn1_g", "bn1_b", "bn1_m", "bn1_v", "dcn_b", "bn2_g", "bn2_b",
                                                  "bn2_m", "bn2_v")], axis=1)
    arrays = {
        "x": a["x"].reshape(B, C, PIX),
        "wqkv": halves(a["L0_conv_w_qkv"].T),
        "wproj": halves(a["L0_conv_w_proj"].T),
        "pos_l": np.concatenate([pos, np.tile(a["L0_conv_b_proj"], (NPOS, 1))[None]], axis=0),
        "pos_r": np.concatenate([a["L1_conv_W"].T, a["L1_conv_b"][None], np.ones((1, C), np.float32)], axis=0),
        "vec": vec.reshape(12, CH, 128).transpose(2, 0, 1),
        "vec64": vec64,
        "w1": halves(a["L2_conv_w1"].T),
        "woff": a["L2_conv_woff"].transpose(1, 2, 3, 0).reshape(CB, 3, 3 * O2),
        "boff": np.tile(a["L2_conv_boff"], (128, 1)),
        "w2": a["L2_conv_w2"].transpose(2, 3, 1, 0).reshape(KK * CB, CB),
        "w3": a["L2_conv_w3"].T,
        "dw": np.stack([a[f"L3_conv_dw{i}"].reshape(CH, 128, 49) for i in (1, 2)]).transpose(2, 0, 1, 3),
        "pw": np.stack([a[f"L3_conv_pw{i}"].reshape(O3, CH, 128).transpose(1, 2, 0) for i in (1, 2)])
              .transpose(2, 0, 1, 3),
        "pwb": np.tile(np.stack([a["L3_conv_pwb1"], a["L3_conv_pwb2"]])[None], (128, 1, 1)),
        "wd": np.stack([a[f"L3_conv_w{i}"].reshape(C, CH, 128, KK).transpose(2, 3, 1, 0) for i in (1, 2)]),
        "ident": ident, "mean32": mean32, "mean8": mean8, "sel2": sel2, "sel3": sel3, "base2": base2,
        "base3": base3,
    }
    arrays = {"in_" + k: np.ascontiguousarray(v) for k, v in arrays.items()}
    nc = bacc.Bacc("TRN2", target_bir_lowering=False, num_devices=1)
    args = [nc.dram_tensor(k, v.shape, mybir.dt.from_np(v.dtype), kind="ExternalInput").ap()
            for k, v in arrays.items()]
    out = nc.dram_tensor("out_y", (B, C, PIX), F32, kind="ExternalOutput").ap()
    order = [k[3:] for k in arrays]
    named = dict(zip(order, args))
    program(nc, out=out, **named)
    got = run_bass_kernel_spmd(nc, [arrays], core_ids=[0])
    return got.results[0]["out_y"].reshape(B, C, H, W)
```
